# Optimizing a Trainium2 kernel written in Bass

```python
import numpy as np
import jax
import jax.numpy as jnp

def _softmax(x, axis=-1):
    return jax.nn.softmax(x, axis=axis)

def _gelu(x):
    return jax.nn.gelu(x, approximate=True)

def _silu(x):
    return jax.nn.silu(x)

def _sigmoid(x):
    return jax.nn.sigmoid(x)

def _layernorm(x, axis=-1, eps=1e-05):
    m = jnp.mean(x, axis=axis, keepdims=True)
    v = jnp.var(x, axis=axis, keepdims=True)
    return (x - m) / jnp.sqrt(v + eps)

def _scatter_add(tgt, idx, src, axis=0):
    return tgt.at[idx].add(src)

def _segment_sum(src, seg, n):
    return jax.ops.segment_sum(src, seg, n)
kernel_name = 'mk_adj_resnorm_d1_adj_r2_393dea'

def setup_inputs(seed: int=0):
    np.random.seed(seed)
    _w = jnp.asarray

    def _rec_inputs():
        import jax
        import jax.numpy as jnp
        _gk = jax.random.key(seed)
        x = 7.22e-05 + 1 * jax.random.normal(jax.random.fold_in(_gk, 1), (4096, 512), jnp.float32)
        _w = (1.0 + jnp.arange(4096, dtype=jnp.float32)) ** (-0.5)
        _w = _w / _w.mean()
        _pij = jnp.clip(0.00195312 * _w[:, None] * _w[None, :], 0.0, 1.0)
        _a = jax.random.uniform(jax.random.fold_in(_gk, 2), (4096, 4096)) < _pij
        _af = _a.astype(jnp.float32)
        adj = _af
        return (x, adj)
    x, adj = _rec_inputs()

    def _L0_gnn_setup():
        import jax, jax.numpy as jnp
        import numpy as np
        N = 4096
        D = 512
        key = jax.random.key(seed)
        ks = jax.random.split(key, 13)
        w_scale = 1.0 / np.sqrt(D)
        inp = {'query': jax.random.normal(ks[0], (N, D), dtype=jnp.float32), 'key': jax.random.normal(ks[1], (N, D), dtype=jnp.float32), 'value': jax.random.normal(ks[2], (N, D), dtype=jnp.float32), 'adj_matrix': jax.random.randint(ks[3], (N, N), 0, 2).astype(jnp.float32), 'Wq': jax.random.normal(ks[4], (D, D), dtype=jnp.float32) * w_scale, 'bq': jax.random.normal(ks[5], (D,), dtype=jnp.float32) * 0.01, 'Wk': jax.random.normal(ks[6], (D, D), dtype=jnp.float32) * w_scale, 'bk': jax.random.normal(ks[7], (D,), dtype=jnp.float32) * 0.01, 'Wv': jax.random.normal(ks[8], (D, D), dtype=jnp.float32) * w_scale, 'bv': jax.random.normal(ks[9], (D,), dtype=jnp.float32) * 0.01, 'Wm': jax.random.normal(ks[10], (D, D), dtype=jnp.float32) * w_scale, 'bm': jax.random.normal(ks[11], (D,), dtype=jnp.float32) * 0.01}
        return inp
    _L0_gnn_all = _L0_gnn_setup()
    _L0_gnn_in = {k: v for k, v in _L0_gnn_all.items() if k in ('key', 'value', 'Wq', 'bq', 'Wk', 'bk', 'Wv', 'bv', 'Wm', 'bm')}
    del _L0_gnn_all
    return {'x': x, 'adj': adj, 'L0_gnn_key': _L0_gnn_in['key'], 'L0_gnn_value': _L0_gnn_in['value'], 'L0_gnn_Wq': _L0_gnn_in['Wq'], 'L0_gnn_bq': _L0_gnn_in['bq'], 'L0_gnn_Wk': _L0_gnn_in['Wk'], 'L0_gnn_bk': _L0_gnn_in['bk'], 'L0_gnn_Wv': _L0_gnn_in['Wv'], 'L0_gnn_bv': _L0_gnn_in['bv'], 'L0_gnn_Wm': _L0_gnn_in['Wm'], 'L0_gnn_bm': _L0_gnn_in['bm']}

def reference(x, adj, L0_gnn_key, L0_gnn_value, L0_gnn_Wq, L0_gnn_bq, L0_gnn_Wk, L0_gnn_bk, L0_gnn_Wv, L0_gnn_bv, L0_gnn_Wm, L0_gnn_bm):
    import jax
    import jax.numpy as jnp

    def _L0_gnn_ref(query, key, value, adj_matrix, Wq, bq, Wk, bk, Wv, bv, Wm, bm):
        import jax, jax.numpy as jnp
        import numpy as np
        N = 4096
        D = 512
        q = query @ Wq.T + bq
        k = key @ Wk.T + bk
        v = value @ Wv.T + bv
        scale = q.shape[0] ** 0.5
        scores = jnp.einsum('nd,md->nm', q, k) / scale
        adj_scores = scores * adj_matrix
        adj_scores = jnp.where(jnp.abs(adj_scores) < 1e-05, -1000000000.0, adj_scores)
        prob = jax.nn.softmax(adj_scores, axis=-1)
        x = jnp.einsum('nm,md->nd', prob, v)
        return x @ Wm.T + bm
    x = _layernorm(x + _L0_gnn_ref(x, L0_gnn_key, L0_gnn_value, adj, L0_gnn_Wq, L0_gnn_bq, L0_gnn_Wk, L0_gnn_bk, L0_gnn_Wv, L0_gnn_bv, L0_gnn_Wm, L0_gnn_bm), axis=-1)
    return x

_drawn_inputs = setup_inputs


def setup_inputs(seed=0):
    import zlib

    import numpy as np

    out = dict(_drawn_inputs(seed))
    spreads = {}
    factors = {'L0_gnn_bq': 44.534, 'L0_gnn_bk': 64.0, 'L0_gnn_bv': 6.472, 'L0_gnn_bm': 6.027}
    for name, (base, spread) in spreads.items():
        noise = np.random.default_rng([zlib.crc32(name.encode()), seed]).standard_normal(out[name].shape)
        drawn = base * np.exp(spread * noise) if base else spread * noise
        out[name] = jnp.asarray(drawn.astype(out[name].dtype))
    for name, factor in factors.items():
        out[name] = (out[name] * factor).astype(out[name].dtype)
    return out
```

```python
from contextlib import ExitStack

import numpy as np

import concourse.bass as bass
from concourse import mybir

F32 = mybir.dt.float32
F16 = mybir.dt.float16
I32 = mybir.dt.int32
ALU = mybir.AluOpType
ACT = mybir.ActivationFunctionType
AX_X = mybir.AxisListType.X

P = 128
BANK = 512


def attention_resnorm(nc, x, adj, key, value, wq, bq, wk, bk, wv, bv, wm, bm, out):
    N, D = x.shape
    T = N // P
    KD = D // P
    C = N // BANK
    TC = BANK // P
    RING = 4
    E = 4
    EC = C // E
    EW = N // E
    WS = 64.0
    PS = 4096.0
    TO_SCORE = 1.0 / (WS * float(N) ** 0.5)
    NEAR_ZERO = 1e-5 / TO_SCORE
    PENALTY = -1e9 / TO_SCORE
    EPS = 1e-5
    LN = 18
    RSQRT_SEED = float(0x5F3759DF)
    assert D == BANK and N % (2 * P) == 0 and KD == TC and C % RING == 0

    with ExitStack() as ctx:
        def sb(name, shape, dt):
            return ctx.enter_context(nc.sbuf_tensor(name, shape, dt))

        def sem(name):
            return ctx.enter_context(nc.semaphore(name))

        k_hi = sb("k_hi", [P, KD, N], F16)
        k_lo = sb("k_lo", [P, KD, N], F16)
        v_slots = sb("v_slots", [P, T + 1, 2, D], F16)
        scores = [sb(f"scores{i}", [P, N], F32) for i in range(2)]
        adj_in = sb("adj_in", [P, RING, BANK], F32)
        a_hi = sb("a_hi", [P, KD, D], F16)
        a_lo = sb("a_lo", [P, KD, D], F16)
        m_hi = sb("m_hi", [P, KD, D], F16)
        m_lo = sb("m_lo", [P, KD, D], F16)
        q_hi = sb("q_hi", [P, KD, P], F16)
        q_lo = sb("q_lo", [P, KD, P], F16)
        xt_hi = sb("xt_hi", [P, KD, P], F16)
        xt_lo = sb("xt_lo", [P, KD, P], F16)
        pt_hi = sb("pt_hi", [P, 2, BANK], F16)
        pt_lo = sb("pt_lo", [P, 2, BANK], F16)
        ot_hi = sb("ot_hi", [P, KD, P], F16)
        ot_lo = sb("ot_lo", [P, KD, P], F16)
        x_query = sb("x_query", [P, D], F32)
        x_res = sb("x_res", [P, D], F32)
        row = sb("row", [P, D], F32)
        out_bias = sb("out_bias", [P, D], F32)
        penalty = sb("penalty", [P, BANK], F32)
        ident = sb("ident", [P, P], F32)
        bias_cols = sb("bias_cols", [P, 3, KD], F32)
        q_bias = sb("q_bias", [P, KD], F32)
        u_hi = sb("u_hi", [P, KD], F16)
        u_lo = sb("u_lo", [P, KD], F16)
        u_f = sb("u_f", [P, KD], F32)
        score_const = sb("score_const", [P, 1], F32)
        score_add = sb("score_add", [P, 1], F32)
        chunk_max = sb("chunk_max", [P, C], F32)
        neg_max = sb("neg_max", [P, 1], F32)
        part_sum = sb("part_sum", [P, E], F32)
        den = sb("den", [P, 3], F32)
        stats = sb("stats", [P, 6], F32)
        mean_var = sb("mean_var", [P, 2], F32)
        rs = sb("rs", [P, 4], F32)
        rs_bits = sb("rs_bits", [P, 2], I32)

        ps = [ctx.enter_context(nc.psum_tensor(f"bank{i}", [P, BANK], F32)) for i in range(8)]
        SCORE, PT, O, X, Y, SMALL = 0, 2, 4, 5, 6, 7

        wq_sb = scores[0][:, 0:KD * D].rearrange("p (k d) -> p k d", k=KD)
        wk_sb = scores[0][:, KD * D:2 * KD * D].rearrange("p (k d) -> p k d", k=KD)
        wv_sb = scores[1][:, 0:KD * D].rearrange("p (k d) -> p k d", k=KD)
        wm_sb = scores[1][:, KD * D:2 * KD * D].rearrange("p (k d) -> p k d", k=KD)
        spread = pt_hi[:, :, :].rearrange("p a b -> p (a b)").bitcast(F32).rearrange(
            "p (k n) -> p k n", k=KD)
        bm_row = pt_lo[0:1, :, :].rearrange("p a b -> p (a b)").bitcast(F32)
        ones_row = row[0:1, 0:P]

        def raw(j0, j1):
            return v_slots[:, j0 + 1:j1 + 1, :, :].rearrange("p t a d -> p (t a d)").bitcast(
                F32).rearrange("p (t d) -> p t d", d=D)

        s_wqk = sem("wq_wk_loaded")
        s_wvm = sem("wv_wm_loaded")
        s_bias = sem("biases_loaded")
        s_key = [sem(f"key_loaded{g}") for g in range(C)]
        s_val = [sem(f"value_loaded{g}") for g in range(C)]
        s_adj = [sem(f"adj_loaded{i}") for i in range(RING)]
        s_xq = sem("x_query_loaded")
        s_xr = sem("x_res_loaded")
        s_out = sem("out_stored")
        s_ident0 = sem("ident_zeroed")
        s_ident = sem("ident_ready")
        s_fill = sem("spread_filled")
        s_spread = sem("spread_ready")
        s_small_ps = sem("small_vectors_in_psum")
        s_small = sem("small_vectors_ready")
        s_a_ps = sem("a_in_psum")
        s_a_hi = sem("a_hi_ready")
        s_a_lo = sem("a_lo_ready")
        s_key_ps = sem("key_tile_in_psum")
        s_k_hi = sem("k_hi_ready")
        s_k_lo = sem("k_lo_ready")
        s_wmt_ps = sem("wm_transposed_in_psum")
        s_wmt = sem("wm_transposed_ready")
        s_m_ps = sem("m_in_psum")
        s_m_hi = sem("m_hi_ready")
        s_m_lo = sem("m_lo_ready")
        s_ob = sem("out_bias_ready")
        s_v_hi = sem("v_hi_ready")
        s_v_lo = sem("v_lo_ready")
        s_xt_ps = sem("x_transposed_in_psum")
        s_xt_hi = sem("xt_hi_ready")
        s_xt_lo = sem("xt_lo_ready")
        s_q_ps = sem("q_in_psum")
        s_q_hi = sem("q_hi_ready")
        s_q_lo = sem("q_lo_ready")
        s_add = sem("score_add_ready")
        s_sc_ps = sem("scores_in_psum")
        s_sc = sem("scores_taken")
        s_abs = sem("abs_ready")
        s_pen = sem("penalty_ready")
        s_masked = sem("scores_masked")
        s_max = sem("max_ready")
        s_exp = sem("exp_ready")
        s_pt_ps = sem("p_transposed_in_psum")
        s_pt_hi = sem("pt_hi_ready")
        s_pt_lo = sem("pt_lo_ready")
        s_pv = sem("pv_chunk_done")
        s_den = sem("denominator_steps")
        s_row = sem("attention_row_ready")
        s_ot_ps = sem("o_transposed_in_psum")
        s_ot_hi = sem("ot_hi_ready")
        s_ot_lo = sem("ot_lo_ready")
        s_y_ps = sem("projection_in_psum")
        s_ln = [sem(f"layernorm_step{i}") for i in range(LN)]

        def need(eng, s, count):
            if not isinstance(count, int) or count > 0:
                eng.wait_ge(s, count)

        def rows_of(dram, t):
            return dram[bass.ds(t * P, P), :]

        block = ctx.enter_context(nc.Block())

        @block.sync
        def _(sp):
            def load_weights(w, dst, s):
                sp.dma_start(dst, w.rearrange("(k p) d -> p k d", p=P)).then_inc(s, 16)

            def load_adj(t, c):
                need(sp, s_sc, t * C + c - RING + 1)
                sp.dma_start(adj_in[:, c % RING, :], adj[bass.ds(t * P, P), c * BANK:(c + 1) * BANK]
                             ).then_inc(s_adj[c % RING], 16)

            def load_x_query(t):
                need(sp, s_xt_ps, t)
                sp.dma_start(x_query[:], rows_of(x, t)).then_inc(s_xq, 16)

            def load_x_res(t):
                need(sp, s_ln[0], t)
                sp.dma_start(x_res[:], rows_of(x, t)).then_inc(s_xr, 16)

            def store(t):
                sp.wait_ge(s_ln[-1], t + 1)
                sp.dma_start(rows_of(out, t), row[:]).then_inc(s_out, 16)

            load_weights(wq, wq_sb, s_wqk)
            load_weights(wk, wk_sb, s_wqk)
            for n, b in enumerate((bq, bk, bv)):
                sp.dma_start(bias_cols[:, n, :], b.rearrange("(k p) -> p k", p=P),
                             allow_slow_non_contiguous=True).then_inc(s_bias, 16)
            sp.dma_start(bm_row, bm.rearrange("(a d) -> a d", a=1)).then_inc(s_bias, 16)
            load_x_query(0)
            for g in range(C):
                sp.dma_start(raw(g * TC, (g + 1) * TC), key[g * BANK:(g + 1) * BANK, :].rearrange(
                    "(t p) d -> p t d", p=P)).then_inc(s_key[g], 16)
                if g < RING:
                    load_adj(0, g)
            load_weights(wv, wv_sb, s_wvm)
            load_weights(wm, wm_sb, s_wvm)
            for g in range(C):
                sp.wait_ge(s_key_ps, (g + 1) * TC)
                sp.dma_start(raw(g * TC, (g + 1) * TC), value[g * BANK:(g + 1) * BANK, :].rearrange(
                    "(t p) d -> p t d", p=P)).then_inc(s_val[g], 16)
                if g + RING < C:
                    load_adj(0, g + RING)
            load_x_query(1)
            load_x_res(0)

            def step(s):
                for c in range(C):
                    load_adj(s, c)
                load_x_query(s + 1)
                if not isinstance(s, int) or s >= 2:
                    store(s - 2)
                    load_x_res(s - 1)

            step(1)
            with sp.Fori(2, T - 2, 2) as s:
                step(s)
                step(s + 1)
            step(T - 2)
            for c in range(C):
                load_adj(T - 1, c)
            for t in range(T - 3, T):
                store(t)
                if t < T - 1:
                    load_x_res(t + 1)
            sp.wait_ge(s_out, T * 16)

        @block.gpsimd
        def _(pool):
            pool.memset(ident[:], 0.0).then_inc(s_ident0, 1)
            pool.wait_ge(s_ident0, 1)
            pool.affine_select(out=ident[:], in_=ident[:], compare_op=ALU.not_equal, fill=1.0,
                               base=0, pattern=[[-1, P]], channel_multiplier=1).then_inc(s_ident, 1)

        @block.tensor
        def _(pe):
            def transpose_blocks(bank, src, s):
                for k in range(KD):
                    last = pe.transpose(ps[bank][:, k * P:(k + 1) * P], src[:, k * P:(k + 1) * P], ident[:])
                last.then_inc(s, 1)

            def products(dst, pairs, first=True, last=True):
                for n, (lh, ll, rh, rl) in enumerate(pairs):
                    pe.matmul(dst, lh, rh, start=first and n == 0, stop=False)
                    pe.matmul(dst, lh, rl, start=False, stop=False)
                    ins = pe.matmul(dst, ll, rh, start=False, stop=last and n == len(pairs) - 1)
                return ins

            def small_vectors():
                pe.wait_ge(s_wqk, 32)
                pe.wait_ge(s_bias, 64)
                for col, (w, b) in enumerate(((wk_sb, 0), (wq_sb, 1))):
                    for d in range(KD):
                        dst = ps[SMALL][:, col * KD + d:col * KD + d + 1]
                        for k in range(KD):
                            pe.matmul(dst, w[:, k, d * P:(d + 1) * P], bias_cols[:, b, k:k + 1],
                                      start=k == 0, stop=k == KD - 1)
                pe.wait_ge(s_spread, 2)
                for k in range(KD):
                    ins = pe.matmul(ps[SMALL][:, 2 * KD:2 * KD + 1], spread[:, k, :],
                                    bias_cols[:, 1, k:k + 1], start=k == 0, stop=k == KD - 1)
                ins.then_inc(s_small_ps, 1)

            def weight_product(banks, left, right, s):
                for d in range(KD):
                    for k in range(KD):
                        ins = pe.matmul(ps[banks[d]][:], left[:, k, d * P:(d + 1) * P], right[:, k, :],
                                        start=k == 0, stop=k == KD - 1)
                    ins.then_inc(s, 1)

            def key_tiles(g):
                pe.wait_ge(s_key[g], 16)
                for j in range(g * TC, (g + 1) * TC):
                    need(pe, s_k_lo, j - 1)
                    transpose_blocks(PT + j % 2, raw(j, j + 1)[:, 0, :], s_key_ps)

            def transpose_x(t):
                pe.wait_ge(s_xq, t * 16 + 16)
                transpose_blocks(X, x_query[:], s_xt_ps)

            def query(t):
                pe.wait_ge(s_xt_hi, t + 1)
                pe.wait_ge(s_xt_lo, t + 1)
                for d in range(KD):
                    cut = slice(d * P, (d + 1) * P)
                    products(ps[Y][:, cut], [(a_hi[:, k, cut], a_lo[:, k, cut], xt_hi[:, k, :], xt_lo[:, k, :])
                                             for k in range(KD)])
                products(ps[SMALL][:, 0:1], [(xt_hi[:, k, :], xt_lo[:, k, :], u_hi[:, k:k + 1], u_lo[:, k:k + 1])
                                             for k in range(KD)]).then_inc(s_q_ps, 1)

            def score_chunk(t, c):
                if c == 0:
                    pe.wait_ge(s_q_hi, t * KD + KD)
                    pe.wait_ge(s_q_lo, t * KD + KD)
                    pe.wait_ge(s_add, t + 1)
                need(pe, s_sc, t * C + c - 1)
                cut = slice(c * BANK, (c + 1) * BANK)
                products(ps[SCORE + c % 2][:], [(q_hi[:, k, :], q_lo[:, k, :], k_hi[:, k, cut], k_lo[:, k, cut])
                                                for k in range(KD)]).then_inc(s_sc_ps, 1)

            def transpose_p(t, par, c):
                need(pe, s_exp, t * E + c // EC + 1)
                need(pe, s_pt_lo, t * C + c - 1)
                transpose_blocks(PT + c % 2, scores[par][:, c * BANK:(c + 1) * BANK], s_pt_ps)

            def pv_chunk(t, c):
                if c == 0:
                    need(pe, s_row, t)
                pe.wait_ge(s_pt_hi, t * C + c + 1)
                pe.wait_ge(s_pt_lo, t * C + c + 1)
                products(ps[O][:], [(pt_hi[:, c % 2, i * P:(i + 1) * P], pt_lo[:, c % 2, i * P:(i + 1) * P],
                                     v_slots[:, c * TC + i, 0, :], v_slots[:, c * TC + i, 1, :])
                                    for i in range(TC)], c == 0, c == C - 1).then_inc(s_pv, 1)

            def transpose_o(t):
                pe.wait_ge(s_row, t + 1)
                transpose_blocks(X, row[:], s_ot_ps)

            def project(t):
                pe.wait_ge(s_ot_hi, t + 1)
                pe.wait_ge(s_ot_lo, t + 1)
                products(ps[Y][:], [(ot_hi[:, k, :], ot_lo[:, k, :], m_hi[:, k, :], m_lo[:, k, :])
                                    for k in range(KD)]).then_inc(s_y_ps, 1)

            def score_phase(t, out_tile):
                for c in range(C):
                    score_chunk(t, c)
                    if out_tile is not None and c == 0:
                        transpose_o(out_tile)
                    if out_tile is not None and c == 2:
                        project(out_tile)

            def pv_phase(t, par, next_tile, out_tile):
                transpose_p(t, par, 0)
                for c in range(C):
                    if c + 1 < C:
                        transpose_p(t, par, c + 1)
                    pv_chunk(t, c)
                    if next_tile is not None and c == 0:
                        transpose_x(next_tile)
                    if next_tile is not None and c == 3:
                        if out_tile is not None:
                            pe.wait_ge(s_ln[0], out_tile + 1)
                        query(next_tile)

            pe.wait_ge(s_ident, 1)
            small_vectors()
            weight_product([0, 1, 2, 3], wq_sb, wk_sb, s_a_ps)
            transpose_x(0)
            pe.wait_ge(s_a_hi, KD)
            pe.wait_ge(s_a_lo, KD)
            pe.wait_ge(s_small, 5)
            key_tiles(0)
            query(0)
            for c in range(C):
                if c + 1 < C:
                    key_tiles(c + 1)
                pe.wait_ge(s_k_hi, (c + 1) * TC)
                pe.wait_ge(s_k_lo, (c + 1) * TC)
                score_chunk(0, c)
            pe.wait_ge(s_wvm, 32)
            m_banks = [PT, PT + 1, O, X]
            for f in range(KD):
                for k in range(KD):
                    ins = pe.transpose(ps[m_banks[f]][:, k * P:(k + 1) * P], wm_sb[:, k, f * P:(f + 1) * P], ident[:])
                ins.then_inc(s_wmt_ps, 1)
            pe.wait_ge(s_wmt, KD)
            pe.wait_ge(s_spread, 3)
            for k in range(KD):
                pe.matmul(ps[Y][:], spread[:, k, :], wm_sb[:, k, :], start=k == 0, stop=False)
            pe.matmul(ps[Y][:], ones_row, bm_row, start=False, stop=True).then_inc(s_m_ps, 1)
            weight_product(m_banks, wv_sb, wm_sb, s_m_ps)
            pe.wait_ge(s_m_hi, KD)
            pe.wait_ge(s_m_lo, KD)
            pe.wait_ge(s_ob, 1)
            transpose_x(1)
            query(1)
            score_phase(1, None)
            pe.wait_ge(s_v_hi, T)
            pe.wait_ge(s_v_lo, T)
            pv_phase(0, 0, 2, None)
            with pe.Fori(2, T - 2, 2) as s:
                for i in range(2):
                    score_phase(s + i, s + i - 2)
                    pv_phase(s + i - 1, 1 - i, s + i + 1, s + i - 2)
            score_phase(T - 2, T - 4)
            pv_phase(T - 3, 1, T - 1, T - 4)
            score_phase(T - 1, T - 3)
            pv_phase(T - 2, 0, None, None)
            transpose_o(T - 2)
            pe.wait_ge(s_ln[0], T - 2)
            project(T - 2)
            pv_phase(T - 1, 1, None, None)
            transpose_o(T - 1)
            pe.wait_ge(s_ln[0], T - 1)
            project(T - 1)

        @block.scalar
        def _(act):
            def hi_key(j):
                act.wait_ge(s_key_ps, j + 1)
                act.activation(k_hi[:, :, j * P:(j + 1) * P], ps[PT + j % 2][:].rearrange("p (k n) -> p k n", k=KD),
                               ACT.Copy).then_inc(s_k_hi, 1)

            def hi_value(j):
                act.wait_ge(s_val[j // TC], 16)
                need(act, s_v_lo, j)
                act.activation(v_slots[:, j, 0, :], raw(j, j + 1)[:, 0, :], ACT.Copy).then_inc(s_v_hi, 1)

            def hi_x(t):
                act.wait_ge(s_xt_ps, t + 1)
                need(act, s_q_ps, t)
                act.activation(xt_hi[:], ps[X][:].rearrange("p (k n) -> p k n", k=KD), ACT.Copy).then_inc(s_xt_hi, 1)

            def hi_query(t):
                act.wait_ge(s_q_ps, t + 1)
                need(act, s_sc_ps, t * C)
                for d in range(KD):
                    act.activation(q_hi[:, d, :], ps[Y][:, d * P:(d + 1) * P], ACT.Identity,
                                   bias=q_bias[:, d:d + 1]).then_inc(s_q_hi, 1)

            def abs_scores(t, par, c):
                act.wait_ge(s_sc, t * C + c + 1)
                need(act, s_masked, t * C + c)
                act.activation(penalty[:], scores[par][:, c * BANK:(c + 1) * BANK], ACT.Abs).then_inc(s_abs, 1)

            def exp_piece(t, par, e):
                act.wait_ge(s_max, t + 1)
                if e == 0:
                    need(act, s_den, t * 3 - 2)
                cut = scores[par][:, e * EW:(e + 1) * EW]
                act.activation(cut, cut, ACT.Exp, bias=neg_max[:, 0:1],
                               accum_out=part_sum[:, e:e + 1]).then_inc(s_exp, 1)

            def hi_p(t, c):
                act.wait_ge(s_pt_ps, t * C + c + 1)
                need(act, s_pv, t * C + c - 1)
                act.activation(pt_hi[:, c % 2, :], ps[PT + c % 2][:], ACT.Copy, scale=PS).then_inc(s_pt_hi, 1)

            def attention_row(t):
                act.wait_ge(s_pv, t * C + C)
                act.wait_ge(s_den, t * 3 + 3)
                need(act, s_out, t * 16)
                act.activation(row[:], ps[O][:], ACT.Copy, scale=den[:, 2:3]).then_inc(s_row, 1)

            def hi_o(t):
                act.wait_ge(s_ot_ps, t + 1)
                act.activation(ot_hi[:], ps[X][:].rearrange("p (k n) -> p k n", k=KD), ACT.Copy).then_inc(s_ot_hi, 1)

            def score_phase(t, par, out_tile):
                for c in range(C):
                    abs_scores(t, par, c)
                    if out_tile is not None and c == 0:
                        hi_o(out_tile)

            def pv_phase(t, next_par, next_tile):
                for c in range(C):
                    hi_p(t, c)
                    if c == 1:
                        yield "x"
                    if c == 4:
                        yield "q"
                    if next_tile is not None and c % EC == 1:
                        exp_piece(next_tile, next_par, c // EC)
                attention_row(t)

            def run_pv(t, par, next_tile, query_tile):
                for what in pv_phase(t, 1 - par, next_tile):
                    if query_tile is not None:
                        (hi_x if what == "x" else hi_query)(query_tile)

            for d in range(KD):
                act.wait_ge(s_a_ps, d + 1)
                act.activation(a_hi[:, d, :], ps[d][:], ACT.Copy, scale=WS).then_inc(s_a_hi, 1)
            hi_x(0)
            for j in range(TC):
                hi_key(j)
            act.wait_ge(s_small, 1)
            hi_query(0)
            for c in range(C):
                if c + 1 < C:
                    for j in range((c + 1) * TC, (c + 2) * TC):
                        hi_key(j)
                abs_scores(0, 0, c)
            for f, bank in enumerate([PT, PT + 1, O, X]):
                act.wait_ge(s_wmt_ps, KD)
                act.activation(wm_sb[:, f, :], ps[bank][:], ACT.Copy).then_inc(s_wmt, 1)
            for e in range(E):
                exp_piece(0, 0, e)
            for j in range(T // 2):
                hi_value(j)
            for d, bank in enumerate([PT, PT + 1, O, X]):
                act.wait_ge(s_m_ps, d + 2)
                act.activation(m_hi[:, d, :], ps[bank][:], ACT.Copy, scale=WS).then_inc(s_m_hi, 1)
            hi_x(1)
            hi_query(1)
            for c in range(C):
                abs_scores(1, 1, c)
                for j in range((T // 2) + 2 * c, (T // 2) + 2 * c + 2):
                    hi_value(j)
            run_pv(0, 0, 1, 2)
            with act.Fori(2, T - 2, 2) as s:
                for i in range(2):
                    score_phase(s + i, i, s + i - 2)
                    run_pv(s + i - 1, 1 - i, s + i, s + i + 1)
            score_phase(T - 2, 0, T - 4)
            run_pv(T - 3, 1, T - 2, T - 1)
            score_phase(T - 1, 1, T - 3)
            run_pv(T - 2, 0, T - 1, None)
            hi_o(T - 2)
            run_pv(T - 1, 1, None, None)
            hi_o(T - 1)

        @block.vector
        def _(dve):
            def lo_key(j):
                dve.wait_ge(s_k_hi, j + 1)
                cut = slice(j * P, (j + 1) * P)
                dve.tensor_tensor(k_lo[:, :, cut], ps[PT + j % 2][:].rearrange("p (k n) -> p k n", k=KD),
                                  k_hi[:, :, cut], ALU.subtract).then_inc(s_k_lo, 1)

            def lo_value(j):
                dve.wait_ge(s_v_hi, j + 1)
                dve.tensor_tensor(v_slots[:, j, 1, :], raw(j, j + 1)[:, 0, :], v_slots[:, j, 0, :],
                                  ALU.subtract).then_inc(s_v_lo, 1)

            def lo_weights(hi, lo, d, bank, s_hi, s_lo):
                dve.wait_ge(s_hi, d + 1)
                dve.scalar_tensor_tensor(lo[:, d, :], ps[bank][:], WS, hi[:, d, :], ALU.mult,
                                         ALU.subtract).then_inc(s_lo, 1)

            def lo_x(t):
                dve.wait_ge(s_xt_hi, t + 1)
                dve.tensor_tensor(xt_lo[:], ps[X][:].rearrange("p (k n) -> p k n", k=KD), xt_hi[:],
                                  ALU.subtract).then_inc(s_xt_lo, 1)

            def lo_query(t):
                dve.wait_ge(s_q_hi, t * KD + KD)
                for d in range(KD):
                    dve.scalar_tensor_tensor(q_lo[:, d, :], ps[Y][:, d * P:(d + 1) * P], q_bias[:, d:d + 1],
                                             q_hi[:, d, :], ALU.add, ALU.subtract).then_inc(s_q_lo, 1)
                dve.tensor_tensor(score_add[:], ps[SMALL][:, 0:1], score_const[:], ALU.add).then_inc(s_add, 1)

            def take_scores(t, par, c):
                if c == 0:
                    dve.wait_ge(s_add, t + 1)
                    need(dve, s_pt_ps, (t - 1) * C)
                dve.wait_ge(s_sc_ps, t * C + c + 1)
                dve.wait_ge(s_adj[c % RING], t * (C // RING * 16) + (c // RING + 1) * 16)
                dve.scalar_tensor_tensor(scores[par][:, c * BANK:(c + 1) * BANK], ps[SCORE + c % 2][:],
                                         score_add[:, 0:1], adj_in[:, c % RING, :],
                                         ALU.add, ALU.mult).then_inc(s_sc, 1)

            def mask_chunk(t, par, c):
                if c == 0:
                    need(dve, s_max, t)
                cut = scores[par][:, c * BANK:(c + 1) * BANK]
                dve.wait_ge(s_abs, t * C + c + 1)
                dve.tensor_scalar(penalty[:], penalty[:], NEAR_ZERO, PENALTY, ALU.is_lt, ALU.mult).then_inc(s_pen, 1)
                dve.wait_ge(s_add, 1)
                dve.wait_ge(s_pen, t * C + c + 1)
                dve.wait_ge(s_sc, t * C + c + 1)
                dve.tensor_tensor_reduce(out=cut, in0=cut, in1=penalty[:], scale=TO_SCORE, scalar=-3e38,
                                         op0=ALU.add, op1=ALU.max, accum_out=chunk_max[:, c:c + 1]
                                         ).then_inc(s_masked, 1)

            def row_max(t):
                dve.wait_ge(s_masked, t * C + C)
                need(dve, s_exp, t * E)
                dve.tensor_reduce(neg_max[:], chunk_max[:], AX_X, ALU.max, negate=True).then_inc(s_max, 1)

            def denominator(t):
                dve.wait_ge(s_exp, t * E + E)
                need(dve, s_row, t)
                dve.tensor_reduce(den[:, 0:1], part_sum[:], AX_X, ALU.add).then_inc(s_den, 1)
                dve.wait_ge(s_den, t * 3 + 1)
                dve.tensor_scalar(den[:, 1:2], den[:, 0:1], PS, None, ALU.mult).then_inc(s_den, 1)
                dve.wait_ge(s_den, t * 3 + 2)
                dve.reciprocal(den[:, 2:3], den[:, 1:2]).then_inc(s_den, 1)

            def lo_p(t, c):
                dve.wait_ge(s_pt_hi, t * C + c + 1)
                dve.scalar_tensor_tensor(pt_lo[:, c % 2, :], ps[PT + c % 2][:], PS, pt_hi[:, c % 2, :],
                                         ALU.mult, ALU.subtract).then_inc(s_pt_lo, 1)

            def lo_o(t):
                dve.wait_ge(s_ot_hi, t + 1)
                dve.tensor_tensor(ot_lo[:], ps[X][:].rearrange("p (k n) -> p k n", k=KD), ot_hi[:],
                                  ALU.subtract).then_inc(s_ot_lo, 1)

            def layernorm(t):
                done = [0]

                def link(ins):
                    ins.then_inc(s_ln[done[0]], 1)
                    dve.wait_ge(s_add, 1)
                    dve.wait_ge(s_ln[done[0]], t + 1)
                    done[0] += 1

                var, seed, shifted = mean_var[:, 1:2], rs_bits[:, 1:2], rs_bits[:, 0:1]
                veps, half, guess, work = (rs[:, i:i + 1] for i in range(4))
                dve.wait_ge(s_y_ps, t + 1)
                dve.wait_ge(s_xr, t * 16 + 16)
                link(dve.scalar_tensor_tensor(row[:], ps[Y][:], 1.0 / WS, x_res[:], ALU.mult, ALU.add))
                link(dve.tensor_tensor(row[:], row[:], out_bias[:], ALU.add))
                link(dve.bn_stats(stats[:], row[:]))
                link(dve.bn_aggr(mean_var[:], stats[:]))
                link(dve.tensor_scalar(veps, var, EPS, None, ALU.add))
                link(dve.tensor_scalar(half, veps, -0.5, None, ALU.mult))
                link(dve.tensor_scalar(shifted, veps.bitcast(I32), 1, None, ALU.logical_shift_right))
                link(dve.tensor_scalar(seed, shifted, -1.0, RSQRT_SEED, ALU.mult, ALU.add))
                cur = seed.bitcast(F32)
                for _ in range(3):
                    link(dve.tensor_tensor(work, cur, cur, ALU.mult))
                    link(dve.tensor_scalar(work, work, half, 1.5, ALU.mult, ALU.add))
                    link(dve.tensor_tensor(guess, cur, work, ALU.mult))
                    cur = guess
                dve.tensor_scalar(row[:], row[:], mean_var[:, 0:1], guess, ALU.subtract, ALU.mult).then_inc(s_ln[-1], 1)
                assert done[0] + 1 == LN

            def score_phase(t, par, out_tile, values=()):
                for c in range(C):
                    take_scores(t, par, c)
                    if c > 0:
                        mask_chunk(t, par, c - 1)
                    for j in values[c * len(values) // C:(c + 1) * len(values) // C]:
                        lo_value(j)
                    if out_tile is not None and c == 0:
                        lo_o(out_tile)
                    if out_tile is not None and c == 3:
                        layernorm(out_tile)
                mask_chunk(t, par, C - 1)
                row_max(t)

            def pv_phase(t, next_tile):
                for c in range(C):
                    lo_p(t, c)
                    if c == 0:
                        denominator(t)
                    if next_tile is not None and c == 1:
                        lo_x(next_tile)
                    if next_tile is not None and c == 4:
                        lo_query(next_tile)

            def spread_bias(n, filled):
                dve.memset(spread, 1.0).then_inc(s_fill, 1)
                dve.wait_ge(s_fill, filled)
                for k in range(KD):
                    ins = dve.tensor_scalar(spread[:, k, :], spread[:, k, :], bias_cols[:, n, k:k + 1], None, ALU.mult)
                ins.then_inc(s_spread, 1)

            dve.memset(ones_row, 1.0).then_inc(s_spread, 1)
            dve.wait_ge(s_bias, 64)
            spread_bias(0, 1)
            dve.wait_ge(s_small_ps, 1)
            dve.tensor_scalar(q_bias[:], ps[SMALL][:, 0:KD], WS, None, ALU.mult).then_inc(s_small, 1)
            dve.tensor_scalar(u_f[:], ps[SMALL][:, KD:2 * KD], WS, None, ALU.mult).then_inc(s_small, 1)
            dve.tensor_scalar(score_const[:], ps[SMALL][:, 2 * KD:2 * KD + 1], WS, None, ALU.mult).then_inc(s_small, 1)
            dve.wait_ge(s_small, 2)
            dve.tensor_copy(u_hi[:], u_f[:]).then_inc(s_small, 1)
            dve.wait_ge(s_small, 4)
            dve.tensor_tensor(u_lo[:], u_f[:], u_hi[:], ALU.subtract).then_inc(s_small, 1)
            for d in range(KD):
                lo_weights(a_hi, a_lo, d, d, s_a_hi, s_a_lo)
            spread_bias(2, 2)
            lo_x(0)
            for j in range(TC):
                lo_key(j)
            dve.wait_ge(s_small, 3)
            lo_query(0)
            for c in range(C):
                if c + 1 < C:
                    for j in range((c + 1) * TC, (c + 2) * TC):
                        lo_key(j)
                take_scores(0, 0, c)
                if c > 0:
                    mask_chunk(0, 0, c - 1)
            mask_chunk(0, 0, C - 1)
            row_max(0)
            for j in range(T // 2):
                lo_value(j)
            dve.wait_ge(s_m_ps, 1)
            dve.tensor_copy(out_bias[:], ps[Y][:]).then_inc(s_ob, 1)
            for d, bank in enumerate([PT, PT + 1, O, X]):
                lo_weights(m_hi, m_lo, d, bank, s_m_hi, s_m_lo)
            lo_x(1)
            lo_query(1)
            score_phase(1, 1, None, range(T // 2, T))
            pv_phase(0, 2)
            with dve.Fori(2, T - 2, 2) as s:
                for i in range(2):
                    score_phase(s + i, i, s + i - 2)
                    pv_phase(s + i - 1, s + i + 1)
            score_phase(T - 2, 0, T - 4)
            pv_phase(T - 3, T - 1)
            score_phase(T - 1, 1, T - 3)
            pv_phase(T - 2, None)
            lo_o(T - 2)
            layernorm(T - 2)
            pv_phase(T - 1, None)
            lo_o(T - 1)
            layernorm(T - 1)


_INS = ["x", "adj", "L0_gnn_key", "L0_gnn_value", "L0_gnn_Wq", "L0_gnn_bq", "L0_gnn_Wk", "L0_gnn_bk",
        "L0_gnn_Wv", "L0_gnn_bv", "L0_gnn_Wm", "L0_gnn_bm"]


def kernel(**inputs):
    import concourse.bacc as bacc
    from concourse.bass_utils import run_bass_kernel_spmd

    nc = bacc.Bacc("TRN2", target_bir_lowering=False, num_devices=1)
    arrays, args = {}, []
    for name in _INS:
        a = np.ascontiguousarray(inputs[name])
        arrays[f"in_{name}_dram"] = a
        args.append(nc.dram_tensor(f"in_{name}_dram", a.shape, mybir.dt.from_np(a.dtype), kind="ExternalInput").ap())
    out = nc.dram_tensor("out_dram", inputs["x"].shape, F32, kind="ExternalOutput").ap()
    attention_resnorm(nc, *args, out)
    r = run_bass_kernel_spmd(nc, [arrays], core_ids=[0])
    return r.results[0]["out_dram"]
```

```python
from contextlib import ExitStack

import numpy as np

import concourse.bass as bass
from concourse import mybir

F32 = mybir.dt.float32
F16 = mybir.dt.float16
I32 = mybir.dt.int32
ALU = mybir.AluOpType
ACT = mybir.ActivationFunctionType
AX_X = mybir.AxisListType.X

P = 128
BANK = 512


def attention_resnorm(nc, x, adj, key, value, wq, bq, wk, bk, wv, bv, wm, bm, out):
    N, D = x.shape
    T = N // P
    KD = D // P
    C = N // BANK
    TC = BANK // P
    RING = 4
    E = 4
    EC = C // E
    EW = N // E
    WS = 64.0
    PS = 4096.0
    TO_SCORE = 1.0 / (WS * float(N) ** 0.5)
    NEAR_ZERO = 1e-5 / TO_SCORE
    PENALTY = -1e9 / TO_SCORE
    EPS = 1e-5
    LN = 18
    RSQRT_SEED = float(0x5F3759DF)
    assert D == BANK and N % (2 * P) == 0 and KD == TC and C % RING == 0

    with ExitStack() as ctx:
        def sb(name, shape, dt):
            return ctx.enter_context(nc.sbuf_tensor(name, shape, dt))

        def sem(name):
            return ctx.enter_context(nc.semaphore(name))

        k_hi = sb("k_hi", [P, KD, N], F16)
        k_lo = sb("k_lo", [P, KD, N], F16)
        v_slots = sb("v_slots", [P, T + 2, 2, D], F16)
        scores = [sb(f"scores{i}", [P, N], F32) for i in range(2)]
        adj_in = sb("adj_in", [P, RING, BANK], F32)
        a_hi = sb("a_hi", [P, KD, D], F16)
        a_lo = sb("a_lo", [P, KD, D], F16)
        m_hi = sb("m_hi", [P, KD, D], F16)
        m_lo = sb("m_lo", [P, KD, D], F16)
        q_hi = sb("q_hi", [P, KD, P], F16)
        q_lo = sb("q_lo", [P, KD, P], F16)
        xt_hi = sb("xt_hi", [P, KD, P], F16)
        xt_lo = sb("xt_lo", [P, KD, P], F16)
        pt_hi = sb("pt_hi", [P, 2, BANK], F16)
        pt_lo = sb("pt_lo", [P, 2, BANK], F16)
        ot_hi = sb("ot_hi", [P, KD, P], F16)
        ot_lo = sb("ot_lo", [P, KD, P], F16)
        x_query = sb("x_query", [P, D], F32)
        x_res = sb("x_res", [P, D], F32)
        ones_row = sb("ones_row", [1, P], F32)
        out_bias = sb("out_bias", [P, D], F32)
        penalty = sb("penalty", [P, BANK], F32)
        ident = sb("ident", [P, P], F32)
        bias_cols = sb("bias_cols", [P, 3, KD], F32)
        q_bias = sb("q_bias", [P, KD], F32)
        u_hi = sb("u_hi", [P, KD], F16)
        u_lo = sb("u_lo", [P, KD], F16)
        u_f = sb("u_f", [P, KD], F32)
        score_const = sb("score_const", [P, 1], F32)
        score_add = sb("score_add", [P, 1], F32)
        chunk_max = sb("chunk_max", [P, C], F32)
        neg_max = sb("neg_max", [P, 1], F32)
        part_sum = sb("part_sum", [P, E], F32)
        den = sb("den", [P, 3], F32)
        stats = sb("stats", [P, 6], F32)
        mean_var = sb("mean_var", [P, 2], F32)
        rs = sb("rs", [P, 4], F32)
        rs_bits = sb("rs_bits", [P, 2], I32)

        ps = [ctx.enter_context(nc.psum_tensor(f"bank{i}", [P, BANK], F32)) for i in range(8)]
        SCORE, PT, O, X, Y, SMALL = 0, 2, 4, 5, 6, 7
        KEY_BANKS = [PT, PT + 1, O, X]
        M_BANKS = [SCORE, PT, PT + 1, O]

        wq_sb = scores[0][:, 0:KD * D].rearrange("p (k d) -> p k d", k=KD)
        wk_sb = scores[0][:, KD * D:2 * KD * D].rearrange("p (k d) -> p k d", k=KD)
        wv_sb = scores[1][:, 0:KD * D].rearrange("p (k d) -> p k d", k=KD)
        wm_sb = scores[1][:, KD * D:2 * KD * D].rearrange("p (k d) -> p k d", k=KD)
        spread = pt_hi[:, :, :].rearrange("p a b -> p (a b)").bitcast(F32).rearrange(
            "p (k n) -> p k n", k=KD)
        bm_row = pt_lo[0:1, :, :].rearrange("p a b -> p (a b)").bitcast(F32)
        row = v_slots[:, T, :, :].rearrange("p a d -> p (a d)").bitcast(F32)

        def raw(j0, j1):
            return v_slots[:, j0 + 2:j1 + 2, :, :].rearrange("p t a d -> p (t a d)").bitcast(
                F32).rearrange("p (t d) -> p t d", d=D)

        s_wqk = sem("wq_wk_loaded")
        s_wvm = sem("wv_wm_loaded")
        s_bias = sem("biases_loaded")
        s_key = [sem(f"key_loaded{g}") for g in range(C)]
        s_val = [sem(f"value_loaded{g}") for g in range(C)]
        s_adj = [sem(f"adj_loaded{i}") for i in range(RING)]
        s_xq = sem("x_query_loaded")
        s_xr = sem("x_res_loaded")
        s_out = sem("out_stored")
        s_ident0 = sem("ident_zeroed")
        s_ident = sem("ident_ready")
        s_fill = sem("spread_filled")
        s_spread = sem("spread_ready")
        s_small_ps = sem("small_vectors_in_psum")
        s_small = sem("small_vectors_ready")
        s_a_ps = sem("a_in_psum")
        s_a_hi = sem("a_hi_ready")
        s_a_lo = sem("a_lo_ready")
        s_key_ps = sem("key_tile_in_psum")
        s_k_hi = sem("k_hi_ready")
        s_k_lo = sem("k_lo_ready")
        s_wmt_ps = sem("wm_transposed_in_psum")
        s_wmt = sem("wm_transposed_ready")
        s_m_ps = sem("m_in_psum")
        s_m_hi = sem("m_hi_ready")
        s_m_lo = sem("m_lo_ready")
        s_ob_ps = sem("out_bias_in_psum")
        s_ob = sem("out_bias_ready")
        s_v_hi = sem("v_hi_ready")
        s_v_lo = sem("v_lo_ready")
        s_xt_ps = sem("x_transposed_in_psum")
        s_xt_hi = sem("xt_hi_ready")
        s_xt_lo = sem("xt_lo_ready")
        s_q_ps = sem("q_in_psum")
        s_q_hi = sem("q_hi_ready")
        s_q_lo = sem("q_lo_ready")
        s_add = sem("score_add_ready")
        s_sc_ps = sem("scores_in_psum")
        s_sc = sem("scores_taken")
        s_abs = sem("abs_ready")
        s_pen = sem("penalty_ready")
        s_masked = sem("scores_masked")
        s_max = sem("max_ready")
        s_exp = sem("exp_ready")
        s_pt_ps = sem("p_transposed_in_psum")
        s_pt_hi = sem("pt_hi_ready")
        s_pt_lo = sem("pt_lo_ready")
        s_pv = sem("pv_chunk_done")
        s_den = sem("denominator_steps")
        s_row = sem("attention_row_ready")
        s_ot_ps = sem("o_transposed_in_psum")
        s_ot_hi = sem("ot_hi_ready")
        s_ot_lo = sem("ot_lo_ready")
        s_y_ps = sem("projection_in_psum")
        s_ln = [sem(f"layernorm_step{i}") for i in range(LN)]

        def need(eng, s, count):
            if not isinstance(count, int) or count > 0:
                eng.wait_ge(s, count)

        def rows_of(dram, t):
            return dram[bass.ds(t * P, P), :]

        block = ctx.enter_context(nc.Block())

        @block.sync
        def _(sp):
            def load_weights(w, dst, s):
                sp.dma_start(dst, w.rearrange("(k p) d -> p k d", p=P)).then_inc(s, 16)

            def load_adj(t, c):
                need(sp, s_sc, t * C + c - RING + 1)
                sp.dma_start(adj_in[:, c % RING, :], adj[bass.ds(t * P, P), c * BANK:(c + 1) * BANK]
                             ).then_inc(s_adj[c % RING], 16)

            def load_x_query(t):
                need(sp, s_xt_ps, t)
                sp.dma_start(x_query[:], rows_of(x, t)).then_inc(s_xq, 16)

            def load_x_res(t):
                need(sp, s_out, t * 16)
                sp.dma_start(x_res[:], rows_of(x, t)).then_inc(s_xr, 16)

            def store(t):
                sp.wait_ge(s_ln[-1], t + 1)
                sp.dma_start(rows_of(out, t), x_res[:]).then_inc(s_out, 16)

            load_weights(wq, wq_sb, s_wqk)
            load_weights(wk, wk_sb, s_wqk)
            for n, b in enumerate((bq, bk, bv)):
                sp.dma_start(bias_cols[:, n, :], b.rearrange("(k p) -> p k", p=P),
                             allow_slow_non_contiguous=True).then_inc(s_bias, 16)
            sp.dma_start(bm_row, bm.rearrange("(a d) -> a d", a=1)).then_inc(s_bias, 16)
            load_x_query(0)
            for g in range(C):
                sp.dma_start(raw(g * TC, (g + 1) * TC), key[g * BANK:(g + 1) * BANK, :].rearrange(
                    "(t p) d -> p t d", p=P)).then_inc(s_key[g], 16)
                if g < RING:
                    load_adj(0, g)
            load_weights(wv, wv_sb, s_wvm)
            load_weights(wm, wm_sb, s_wvm)
            for g in range(C):
                sp.wait_ge(s_key_ps, (g + 1) * TC)
                sp.dma_start(raw(g * TC, (g + 1) * TC), value[g * BANK:(g + 1) * BANK, :].rearrange(
                    "(t p) d -> p t d", p=P)).then_inc(s_val[g], 16)
                if g + RING < C:
                    load_adj(0, g + RING)
            load_x_query(1)
            load_x_res(0)

            def step(s):
                for c in range(C):
                    load_adj(s, c)
                    if c == RING - 1 and (not isinstance(s, int) or s >= 3):
                        store(s - 3)
                        load_x_res(s - 2)
                if not isinstance(s, int) or s + 1 < T:
                    load_x_query(s + 1)

            for s in range(1, 4):
                step(s)
            with sp.Fori(4, T - 2, 2) as s:
                step(s)
                step(s + 1)
            for s in range(T - 2, T):
                step(s)
            for t in range(T - 3, T):
                store(t)
                if t + 1 < T:
                    load_x_res(t + 1)
            sp.wait_ge(s_out, T * 16)

        @block.gpsimd
        def _(pool):
            pool.memset(ident[:], 0.0).then_inc(s_ident0, 1)
            pool.wait_ge(s_ident0, 1)
            pool.affine_select(out=ident[:], in_=ident[:], compare_op=ALU.not_equal, fill=1.0,
                               base=0, pattern=[[-1, P]], channel_multiplier=1).then_inc(s_ident, 1)
            for j in range(T):
                pool.wait_ge(s_v_hi, j + 1)
                pool.tensor_tensor(v_slots[:, j, 1, :], raw(j, j + 1)[:, 0, :], v_slots[:, j, 0, :],
                                   ALU.subtract).then_inc(s_v_lo, 1)

        @block.tensor
        def _(pe):
            def transpose_blocks(bank, src, s):
                for k in range(KD):
                    last = pe.transpose(ps[bank][:, k * P:(k + 1) * P], src[:, k * P:(k + 1) * P], ident[:])
                last.then_inc(s, 1)

            def products(dst, pairs, first=True, last=True):
                for n, (lh, ll, rh, rl) in enumerate(pairs):
                    pe.matmul(dst, lh, rh, start=first and n == 0, stop=False)
                    pe.matmul(dst, lh, rl, start=False, stop=False)
                    ins = pe.matmul(dst, ll, rh, start=False, stop=last and n == len(pairs) - 1)
                return ins

            def small_vectors():
                pe.wait_ge(s_wqk, 32)
                pe.wait_ge(s_bias, 64)
                for col, (w, b) in enumerate(((wk_sb, 0), (wq_sb, 1))):
                    for d in range(KD):
                        dst = ps[SMALL][:, col * KD + d:col * KD + d + 1]
                        for k in range(KD):
                            pe.matmul(dst, w[:, k, d * P:(d + 1) * P], bias_cols[:, b, k:k + 1],
                                      start=k == 0, stop=k == KD - 1)
                pe.wait_ge(s_spread, 2)
                for k in range(KD):
                    ins = pe.matmul(ps[SMALL][:, 2 * KD:2 * KD + 1], spread[:, k, :],
                                    bias_cols[:, 1, k:k + 1], start=k == 0, stop=k == KD - 1)
                ins.then_inc(s_small_ps, 1)

            def weight_product(banks, left, right, s):
                for d in range(KD):
                    for k in range(KD):
                        ins = pe.matmul(ps[banks[d]][:], left[:, k, d * P:(d + 1) * P], right[:, k, :],
                                        start=k == 0, stop=k == KD - 1)
                    ins.then_inc(s, 1)

            def key_tiles(g):
                pe.wait_ge(s_key[g], 16)
                for j in range(g * TC, (g + 1) * TC):
                    need(pe, s_k_lo, j - 3)
                    transpose_blocks(KEY_BANKS[j % 4], raw(j, j + 1)[:, 0, :], s_key_ps)

            def transpose_x(t):
                pe.wait_ge(s_xq, t * 16 + 16)
                transpose_blocks(X, x_query[:], s_xt_ps)

            def query(t):
                pe.wait_ge(s_xt_hi, t + 1)
                pe.wait_ge(s_xt_lo, t + 1)
                for d in range(KD):
                    cut = slice(d * P, (d + 1) * P)
                    products(ps[Y][:, cut], [(a_hi[:, k, cut], a_lo[:, k, cut], xt_hi[:, k, :], xt_lo[:, k, :])
                                             for k in range(KD)])
                products(ps[SMALL][:, 0:1], [(xt_hi[:, k, :], xt_lo[:, k, :], u_hi[:, k:k + 1], u_lo[:, k:k + 1])
                                             for k in range(KD)]).then_inc(s_q_ps, 1)

            def score_chunk(t, c):
                if c == 0:
                    pe.wait_ge(s_q_hi, t * KD + KD)
                    pe.wait_ge(s_q_lo, t * KD + KD)
                    pe.wait_ge(s_add, t + 1)
                need(pe, s_sc, t * C + c - 1)
                cut = slice(c * BANK, (c + 1) * BANK)
                products(ps[SCORE + c % 2][:], [(q_hi[:, k, :], q_lo[:, k, :], k_hi[:, k, cut], k_lo[:, k, cut])
                                                for k in range(KD)]).then_inc(s_sc_ps, 1)

            def transpose_p(t, par, c):
                need(pe, s_exp, t * E + c // EC + 1)
                need(pe, s_pt_lo, t * C + c - 1)
                transpose_blocks(PT + c % 2, scores[par][:, c * BANK:(c + 1) * BANK], s_pt_ps)

            def pv_chunk(t, c):
                if c == 0:
                    need(pe, s_row, t)
                pe.wait_ge(s_pt_hi, t * C + c + 1)
                pe.wait_ge(s_pt_lo, t * C + c + 1)
                products(ps[O][:], [(pt_hi[:, c % 2, i * P:(i + 1) * P], pt_lo[:, c % 2, i * P:(i + 1) * P],
                                     v_slots[:, c * TC + i, 0, :], v_slots[:, c * TC + i, 1, :])
                                    for i in range(TC)], c == 0, c == C - 1).then_inc(s_pv, 1)

            def transpose_o(t):
                pe.wait_ge(s_row, t + 1)
                transpose_blocks(X, row, s_ot_ps)

            def project(t):
                pe.wait_ge(s_ot_hi, t + 1)
                pe.wait_ge(s_ot_lo, t + 1)
                products(ps[Y][:], [(ot_hi[:, k, :], ot_lo[:, k, :], m_hi[:, k, :], m_lo[:, k, :])
                                    for k in range(KD)]).then_inc(s_y_ps, 1)

            def score_phase(t, pv_par, out_tile):
                for c in range(C):
                    score_chunk(t, c)
                    if out_tile is not None and c == 0:
                        transpose_o(out_tile)
                    if out_tile is not None and c == 2:
                        project(out_tile)
                    if c == C - 2:
                        transpose_p(t - 1, pv_par, 0)
                        transpose_p(t - 1, pv_par, 1)

            def pv_phase(t, par, next_tile, out_tile):
                for c in range(C):
                    if 2 <= c + 1 < C:
                        transpose_p(t, par, c + 1)
                    pv_chunk(t, c)
                    if next_tile is not None and c == 0:
                        transpose_x(next_tile)
                    if next_tile is not None and c == 3:
                        if out_tile is not None:
                            pe.wait_ge(s_ln[0], out_tile + 1)
                        query(next_tile)

            pe.wait_ge(s_ident, 1)
            pe.wait_ge(s_wqk, 32)
            weight_product([0, 1, 2, 3], wq_sb, wk_sb, s_a_ps)
            transpose_x(0)
            small_vectors()
            pe.wait_ge(s_a_hi, KD)
            pe.wait_ge(s_a_lo, KD)
            pe.wait_ge(s_small, 5)
            query(0)
            key_tiles(0)
            for c in range(C):
                if c + 1 < C:
                    key_tiles(c + 1)
                pe.wait_ge(s_k_hi, (c + 1) * TC)
                pe.wait_ge(s_k_lo, (c + 1) * TC)
                score_chunk(0, c)
                if c == C - 2:
                    pe.wait_ge(s_k_lo, T)
                    transpose_x(1)
            pe.wait_ge(s_wvm, 32)
            pe.wait_ge(s_sc, C - 1)
            for f in range(KD):
                for k in range(KD):
                    ins = pe.transpose(ps[M_BANKS[f]][:, k * P:(k + 1) * P],
                                       wm_sb[:, k, f * P:(f + 1) * P], ident[:])
                ins.then_inc(s_wmt_ps, 1)
            query(1)
            pe.wait_ge(s_wmt, KD)
            weight_product(M_BANKS, wv_sb, wm_sb, s_m_ps)
            pe.wait_ge(s_spread, 3)
            pe.wait_ge(s_q_hi, 2 * KD)
            pe.wait_ge(s_q_lo, 2 * KD)
            for k in range(KD):
                pe.matmul(ps[Y][:], spread[:, k, :], wm_sb[:, k, :], start=k == 0, stop=False)
            pe.matmul(ps[Y][:], ones_row[:], bm_row, start=False, stop=True).then_inc(s_ob_ps, 1)
            pe.wait_ge(s_m_lo, 1)
            for c in range(C - 1):
                score_chunk(1, c)
            pe.wait_ge(s_m_hi, KD)
            pe.wait_ge(s_m_lo, KD)
            pe.wait_ge(s_ob, 1)
            transpose_p(0, 0, 0)
            transpose_p(0, 0, 1)
            score_chunk(1, C - 1)
            pe.wait_ge(s_v_hi, T)
            pe.wait_ge(s_v_lo, T)
            pv_phase(0, 0, 2, None)
            with pe.Fori(2, T - 2, 2) as s:
                for i in range(2):
                    score_phase(s + i, 1 - i, s + i - 2)
                    pv_phase(s + i - 1, 1 - i, s + i + 1, s + i - 2)
            score_phase(T - 2, 1, T - 4)
            pv_phase(T - 3, 1, T - 1, T - 4)
            score_phase(T - 1, 0, T - 3)
            pv_phase(T - 2, 0, None, None)
            transpose_o(T - 2)
            pe.wait_ge(s_ln[0], T - 2)
            project(T - 2)
            transpose_p(T - 1, 1, 0)
            transpose_p(T - 1, 1, 1)
            pv_phase(T - 1, 1, None, None)
            transpose_o(T - 1)
            pe.wait_ge(s_ln[0], T - 1)
            project(T - 1)

        @block.scalar
        def _(act):
            def hi_key(j):
                act.wait_ge(s_key_ps, j + 1)
                act.activation(k_hi[:, :, j * P:(j + 1) * P], ps[KEY_BANKS[j % 4]][:].rearrange("p (k n) -> p k n", k=KD),
                               ACT.Copy).then_inc(s_k_hi, 1)

            def hi_value(j):
                act.wait_ge(s_val[j // TC], 16)
                need(act, s_v_lo, j - 1)
                act.activation(v_slots[:, j, 0, :], raw(j, j + 1)[:, 0, :], ACT.Copy).then_inc(s_v_hi, 1)

            def hi_x(t):
                act.wait_ge(s_xt_ps, t + 1)
                need(act, s_q_ps, t)
                act.activation(xt_hi[:], ps[X][:].rearrange("p (k n) -> p k n", k=KD), ACT.Copy).then_inc(s_xt_hi, 1)

            def hi_query(t):
                act.wait_ge(s_q_ps, t + 1)
                need(act, s_sc_ps, t * C)
                for d in range(KD):
                    act.activation(q_hi[:, d, :], ps[Y][:, d * P:(d + 1) * P], ACT.Identity,
                                   bias=q_bias[:, d:d + 1]).then_inc(s_q_hi, 1)

            def abs_scores(t, par, c):
                act.wait_ge(s_sc, t * C + c + 1)
                need(act, s_masked, t * C + c)
                act.activation(penalty[:], scores[par][:, c * BANK:(c + 1) * BANK], ACT.Abs).then_inc(s_abs, 1)

            def exp_piece(t, par, e):
                act.wait_ge(s_max, t + 1)
                if e == 0:
                    need(act, s_den, t * 3 - 2)
                cut = scores[par][:, e * EW:(e + 1) * EW]
                act.activation(cut, cut, ACT.Exp, bias=neg_max[:, 0:1],
                               accum_out=part_sum[:, e:e + 1]).then_inc(s_exp, 1)

            def hi_p(t, c):
                act.wait_ge(s_pt_ps, t * C + c + 1)
                need(act, s_pv, t * C + c - 1)
                act.activation(pt_hi[:, c % 2, :], ps[PT + c % 2][:], ACT.Copy, scale=PS).then_inc(s_pt_hi, 1)

            def attention_row(t):
                act.wait_ge(s_pv, t * C + C)
                act.wait_ge(s_den, t * 3 + 3)
                need(act, s_ot_ps, t)
                act.activation(row, ps[O][:], ACT.Copy, scale=den[:, 2:3]).then_inc(s_row, 1)

            def hi_o(t):
                act.wait_ge(s_ot_ps, t + 1)
                act.activation(ot_hi[:], ps[X][:].rearrange("p (k n) -> p k n", k=KD), ACT.Copy).then_inc(s_ot_hi, 1)

            def score_phase(t, par, out_tile):
                for c in range(C):
                    abs_scores(t, par, c)
                    if out_tile is not None and c == 0:
                        hi_o(out_tile)
                    if c == C - 3:
                        hi_p(t - 1, 0)
                    if c == C - 2:
                        hi_p(t - 1, 1)

            def pv_phase(t, next_par, next_tile):
                for c in range(1, C):
                    if c > 1:
                        hi_p(t, c)
                    if c == 1:
                        yield "x"
                    if c == 4:
                        yield "q"
                    if next_tile is not None and c in (2, 3, 5, 6):
                        exp_piece(next_tile, next_par, (2, 3, 5, 6).index(c))
                attention_row(t)

            def run_pv(t, par, next_tile, query_tile):
                for what in pv_phase(t, 1 - par, next_tile):
                    if query_tile is not None:
                        (hi_x if what == "x" else hi_query)(query_tile)

            for d in range(KD):
                act.wait_ge(s_a_ps, d + 1)
                act.activation(a_hi[:, d, :], ps[d][:], ACT.Copy, scale=WS).then_inc(s_a_hi, 1)
            hi_x(0)
            act.wait_ge(s_small, 1)
            hi_query(0)
            values = iter(range(T))

            def hi_values(n):
                for _, j in zip(range(n), values):
                    hi_value(j)

            for g in range(C):
                for j in range(g * TC, (g + 1) * TC):
                    hi_key(j)
                if g >= 2:
                    hi_values(3)
            hi_x(1)
            hi_query(1)
            for c in range(C):
                abs_scores(0, 0, c)
                hi_values(1)
            for e in range(E):
                exp_piece(0, 0, e)
                hi_values(1)
            hi_values(T)
            for c in range(C):
                abs_scores(1, 1, c)
                if c >= C - 3 and c < C - 1:
                    hi_p(0, c - C + 3)
            run_pv(0, 0, 1, 2)
            with act.Fori(2, T - 2, 2) as s:
                for i in range(2):
                    score_phase(s + i, i, s + i - 2)
                    run_pv(s + i - 1, 1 - i, s + i, s + i + 1)
            score_phase(T - 2, 0, T - 4)
            run_pv(T - 3, 1, T - 2, T - 1)
            score_phase(T - 1, 1, T - 3)
            run_pv(T - 2, 0, T - 1, None)
            hi_o(T - 2)
            hi_p(T - 1, 0)
            hi_p(T - 1, 1)
            run_pv(T - 1, 1, None, None)
            hi_o(T - 1)

        @block.vector
        def _(dve):
            def lo_key(j):
                dve.wait_ge(s_k_hi, j + 1)
                cut = slice(j * P, (j + 1) * P)
                dve.tensor_tensor(k_lo[:, :, cut], ps[KEY_BANKS[j % 4]][:].rearrange("p (k n) -> p k n", k=KD),
                                  k_hi[:, :, cut], ALU.subtract).then_inc(s_k_lo, 1)

            def lo_weights(hi, lo, d, bank, s_hi, s_lo):
                dve.wait_ge(s_hi, d + 1)
                dve.scalar_tensor_tensor(lo[:, d, :], ps[bank][:], WS, hi[:, d, :], ALU.mult,
                                         ALU.subtract).then_inc(s_lo, 1)

            def lo_x(t):
                dve.wait_ge(s_xt_hi, t + 1)
                dve.tensor_tensor(xt_lo[:], ps[X][:].rearrange("p (k n) -> p k n", k=KD), xt_hi[:],
                                  ALU.subtract).then_inc(s_xt_lo, 1)

            def lo_query(t):
                dve.wait_ge(s_q_hi, t * KD + KD)
                for d in range(KD):
                    dve.scalar_tensor_tensor(q_lo[:, d, :], ps[Y][:, d * P:(d + 1) * P], q_bias[:, d:d + 1],
                                             q_hi[:, d, :], ALU.add, ALU.subtract).then_inc(s_q_lo, 1)
                dve.tensor_tensor(score_add[:], ps[SMALL][:, 0:1], score_const[:], ALU.add).then_inc(s_add, 1)

            def take_scores(t, par, c):
                if c == 0:
                    dve.wait_ge(s_add, t + 1)
                    need(dve, s_pt_ps, (t - 1) * C)
                dve.wait_ge(s_sc_ps, t * C + c + 1)
                dve.wait_ge(s_adj[c % RING], t * (C // RING * 16) + (c // RING + 1) * 16)
                dve.scalar_tensor_tensor(scores[par][:, c * BANK:(c + 1) * BANK], ps[SCORE + c % 2][:],
                                         score_add[:, 0:1], adj_in[:, c % RING, :],
                                         ALU.add, ALU.mult).then_inc(s_sc, 1)

            def mask_chunk(t, par, c):
                if c == 0:
                    need(dve, s_max, t)
                cut = scores[par][:, c * BANK:(c + 1) * BANK]
                dve.wait_ge(s_abs, t * C + c + 1)
                dve.tensor_scalar(penalty[:], penalty[:], NEAR_ZERO, PENALTY, ALU.is_lt, ALU.mult).then_inc(s_pen, 1)
                dve.wait_ge(s_add, 1)
                dve.wait_ge(s_pen, t * C + c + 1)
                dve.wait_ge(s_sc, t * C + c + 1)
                dve.tensor_tensor_reduce(out=cut, in0=cut, in1=penalty[:], scale=TO_SCORE, scalar=-3e38,
                                         op0=ALU.add, op1=ALU.max, accum_out=chunk_max[:, c:c + 1]
                                         ).then_inc(s_masked, 1)

            def row_max(t):
                dve.wait_ge(s_masked, t * C + C)
                need(dve, s_exp, t * E)
                dve.tensor_reduce(neg_max[:], chunk_max[:], AX_X, ALU.max, negate=True).then_inc(s_max, 1)

            def denominator(t):
                dve.wait_ge(s_exp, t * E + E)
                need(dve, s_row, t)
                dve.tensor_reduce(den[:, 0:1], part_sum[:], AX_X, ALU.add).then_inc(s_den, 1)
                dve.wait_ge(s_den, t * 3 + 1)
                dve.tensor_scalar(den[:, 1:2], den[:, 0:1], PS, None, ALU.mult).then_inc(s_den, 1)
                dve.wait_ge(s_den, t * 3 + 2)
                dve.reciprocal(den[:, 2:3], den[:, 1:2]).then_inc(s_den, 1)

            def lo_p(t, c):
                dve.wait_ge(s_pt_hi, t * C + c + 1)
                dve.scalar_tensor_tensor(pt_lo[:, c % 2, :], ps[PT + c % 2][:], PS, pt_hi[:, c % 2, :],
                                         ALU.mult, ALU.subtract).then_inc(s_pt_lo, 1)

            def lo_o(t):
                dve.wait_ge(s_ot_hi, t + 1)
                dve.tensor_tensor(ot_lo[:], ps[X][:].rearrange("p (k n) -> p k n", k=KD), ot_hi[:],
                                  ALU.subtract).then_inc(s_ot_lo, 1)

            def after(n, t):
                dve.wait_ge(s_add, 1)
                dve.wait_ge(s_ln[n], t + 1)

            var = mean_var[:, 1:2]
            shifted, seed = rs_bits[:, 0:1], rs_bits[:, 1:2]
            veps, half, guess, work = (rs[:, i:i + 1] for i in range(4))

            def add_residual(t):
                dve.wait_ge(s_y_ps, t + 1)
                dve.wait_ge(s_xr, t * 16 + 16)
                dve.scalar_tensor_tensor(x_res[:], ps[Y][:], 1.0 / WS, x_res[:], ALU.mult,
                                         ALU.add).then_inc(s_ln[0], 1)

            def row_statistics(t):
                after(0, t)
                dve.tensor_tensor(x_res[:], x_res[:], out_bias[:], ALU.add).then_inc(s_ln[1], 1)
                after(1, t)
                dve.bn_stats(stats[:], x_res[:]).then_inc(s_ln[2], 1)

            def rsqrt_guess(t):
                after(2, t)
                dve.bn_aggr(mean_var[:], stats[:]).then_inc(s_ln[3], 1)
                after(3, t)
                dve.tensor_scalar(veps, var, EPS, None, ALU.add).then_inc(s_ln[4], 1)
                after(4, t)
                dve.tensor_scalar(half, veps, -0.5, None, ALU.mult).then_inc(s_ln[5], 1)
                dve.tensor_scalar(shifted, veps.bitcast(I32), 1, None,
                                  ALU.logical_shift_right).then_inc(s_ln[6], 1)
                after(6, t)
                dve.tensor_scalar(seed, shifted, -1.0, RSQRT_SEED, ALU.mult, ALU.add).then_inc(s_ln[7], 1)

            def newton(t, n):
                cur = guess if n else seed.bitcast(F32)
                after(7 + 3 * n, t)
                dve.tensor_tensor(work, cur, cur, ALU.mult).then_inc(s_ln[8 + 3 * n], 1)
                after(8 + 3 * n, t)
                if n == 0:
                    after(5, t)
                dve.tensor_scalar(work, work, half, 1.5, ALU.mult, ALU.add).then_inc(s_ln[9 + 3 * n], 1)
                after(9 + 3 * n, t)
                dve.tensor_tensor(guess, cur, work, ALU.mult).then_inc(s_ln[10 + 3 * n], 1)

            def normalize(t):
                after(LN - 2, t)
                dve.tensor_scalar(x_res[:], x_res[:], mean_var[:, 0:1], guess, ALU.subtract,
                                  ALU.mult).then_inc(s_ln[LN - 1], 1)

            def score_phase(t, par, out_tile):
                for c in range(C):
                    take_scores(t, par, c)
                    if c > 0:
                        mask_chunk(t, par, c - 1)
                    if out_tile is not None and c == 0:
                        lo_o(out_tile)
                    if out_tile is not None and c == 3:
                        add_residual(out_tile)
                    if c >= C - 2:
                        lo_p(t - 1, c - C + 2)
                mask_chunk(t, par, C - 1)
                row_max(t)

            def pv_phase(t, next_tile, out_tile):
                denominator(t)
                for c in range(1, C):
                    if c > 1:
                        lo_p(t, c)
                    if next_tile is not None and c == 1:
                        lo_x(next_tile)
                    if next_tile is not None and c == 4:
                        lo_query(next_tile)
                    if out_tile is not None:
                        if c == 2:
                            row_statistics(out_tile)
                        if c == 3:
                            rsqrt_guess(out_tile)
                        if c >= 5:
                            newton(out_tile, c - 5)
                if out_tile is not None:
                    normalize(out_tile)

            def spread_bias(n, filled):
                dve.memset(spread, 1.0).then_inc(s_fill, 1)
                dve.wait_ge(s_fill, filled)
                for k in range(KD):
                    ins = dve.tensor_scalar(spread[:, k, :], spread[:, k, :], bias_cols[:, n, k:k + 1], None, ALU.mult)
                ins.then_inc(s_spread, 1)

            dve.memset(ones_row[:], 1.0).then_inc(s_spread, 1)
            dve.wait_ge(s_bias, 64)
            spread_bias(0, 1)
            for d in range(KD):
                lo_weights(a_hi, a_lo, d, d, s_a_hi, s_a_lo)
            lo_x(0)
            dve.wait_ge(s_small_ps, 1)
            dve.tensor_scalar(q_bias[:], ps[SMALL][:, 0:KD], WS, None, ALU.mult).then_inc(s_small, 1)
            dve.tensor_scalar(u_f[:], ps[SMALL][:, KD:2 * KD], WS, None, ALU.mult).then_inc(s_small, 1)
            dve.tensor_scalar(score_const[:], ps[SMALL][:, 2 * KD:2 * KD + 1], WS, None, ALU.mult).then_inc(s_small, 1)
            dve.wait_ge(s_small, 2)
            dve.tensor_copy(u_hi[:], u_f[:]).then_inc(s_small, 1)
            dve.wait_ge(s_small, 4)
            dve.tensor_tensor(u_lo[:], u_f[:], u_hi[:], ALU.subtract).then_inc(s_small, 1)
            spread_bias(2, 2)
            lo_query(0)
            for j in range(TC):
                lo_key(j)
            for c in range(C):
                if c + 1 < C:
                    for j in range((c + 1) * TC, (c + 2) * TC):
                        lo_key(j)
                take_scores(0, 0, c)
            lo_x(1)
            dve.wait_ge(s_wmt_ps, KD)
            for f in range(KD):
                dve.tensor_copy(wm_sb[:, f, :], ps[M_BANKS[f]][:]).then_inc(s_wmt, 1)
            lo_query(1)
            for c in range(C):
                mask_chunk(0, 0, c)
            row_max(0)
            for d in range(KD):
                dve.wait_ge(s_m_ps, d + 1)
                dve.tensor_scalar(m_hi[:, d, :], ps[M_BANKS[d]][:], WS, None, ALU.mult).then_inc(s_m_hi, 1)
                lo_weights(m_hi, m_lo, d, M_BANKS[d], s_m_hi, s_m_lo)
            dve.wait_ge(s_ob_ps, 1)
            dve.tensor_copy(out_bias[:], ps[Y][:]).then_inc(s_ob, 1)
            score_phase(1, 1, None)
            pv_phase(0, 2, None)
            with dve.Fori(2, T - 2, 2) as s:
                for i in range(2):
                    score_phase(s + i, i, s + i - 2)
                    pv_phase(s + i - 1, s + i + 1, s + i - 2)
            score_phase(T - 2, 0, T - 4)
            pv_phase(T - 3, T - 1, T - 4)
            score_phase(T - 1, 1, T - 3)
            pv_phase(T - 2, None, T - 3)
            lo_o(T - 2)
            lo_p(T - 1, 0)
            lo_p(T - 1, 1)
            add_residual(T - 2)
            pv_phase(T - 1, None, T - 2)
            lo_o(T - 1)
            add_residual(T - 1)
            row_statistics(T - 1)
            rsqrt_guess(T - 1)
            for n in range(3):
                newton(T - 1, n)
            normalize(T - 1)


_INS = ["x", "adj", "L0_gnn_key", "L0_gnn_value", "L0_gnn_Wq", "L0_gnn_bq", "L0_gnn_Wk", "L0_gnn_bk",
        "L0_gnn_Wv", "L0_gnn_bv", "L0_gnn_Wm", "L0_gnn_bm"]


def kernel(**inputs):
    import concourse.bacc as bacc
    from concourse.bass_utils import run_bass_kernel_spmd

    nc = bacc.Bacc("TRN2", target_bir_lowering=False, num_devices=1)
    arrays, args = {}, []
    for name in _INS:
        a = np.ascontiguousarray(inputs[name])
        arrays[f"in_{name}_dram"] = a
        args.append(nc.dram_tensor(f"in_{name}_dram", a.shape, mybir.dt.from_np(a.dtype), kind="ExternalInput").ap())
    out = nc.dram_tensor("out_dram", inputs["x"].shape, F32, kind="ExternalOutput").ap()
    attention_resnorm(nc, *args, out)
    r = run_bass_kernel_spmd(nc, [arrays], core_ids=[0])
    return r.results[0]["out_dram"]
```

```python
from contextlib import ExitStack

import numpy as np

import concourse.bass as bass
from concourse import mybir

F32 = mybir.dt.float32
F16 = mybir.dt.float16
I32 = mybir.dt.int32
ALU = mybir.AluOpType
ACT = mybir.ActivationFunctionType
AX_X = mybir.AxisListType.X

P = 128
BANK = 512


def attention_resnorm(nc, x, adj, key, value, wq, bq, wk, bk, wv, bv, wm, bm, out):
    N, D = x.shape
    T = N // P
    KD = D // P
    C = N // BANK
    TC = BANK // P
    RING = 4
    E = 2
    EDGES = (0, C // 2, C)
    Q = 32
    G = P // Q
    PARTS = E * G * G
    WS = 64.0
    PS = 4096.0
    TO_SCORE = 1.0 / (WS * float(N) ** 0.5)
    NEAR_ZERO = 1e-5 / TO_SCORE
    PENALTY = -1e9 / TO_SCORE
    EPS = 1e-5
    LN = 15
    RSQRT_SEED = float(0x5F3759DF)
    assert D == BANK and N % (2 * P) == 0 and KD == TC and C % RING == 0

    with ExitStack() as ctx:
        def sb(name, shape, dt):
            return ctx.enter_context(nc.sbuf_tensor(name, shape, dt))

        def sem(name):
            return ctx.enter_context(nc.semaphore(name))

        k_hi = sb("k_hi", [P, KD, N], F16)
        k_lo = sb("k_lo", [P, KD, N], F16)
        v_slots = sb("v_slots", [P, T + 2, 2, D], F16)
        scores = sb("scores", [P, N], F32)
        probs = sb("probs", [P, N], F32)
        adj_in = sb("adj_in", [P, RING, BANK], F32)
        a_hi = sb("a_hi", [P, KD, D], F16)
        a_lo = sb("a_lo", [P, KD, D], F16)
        m_hi = sb("m_hi", [P, KD, D], F16)
        m_lo = sb("m_lo", [P, KD, D], F16)
        q_hi = sb("q_hi", [P, KD, P], F16)
        q_lo = sb("q_lo", [P, KD, P], F16)
        xt_hi = sb("xt_hi", [P, KD, P], F16)
        xt_lo = sb("xt_lo", [P, KD, P], F16)
        pt_hi = sb("pt_hi", [P, 2, BANK], F16)
        pt_lo = sb("pt_lo", [P, 2, BANK], F16)
        ot_hi = sb("ot_hi", [P, KD, P], F16)
        ot_lo = sb("ot_lo", [P, KD, P], F16)
        x_query = sb("x_query", [P, D], F32)
        x_res = sb("x_res", [P, D], F32)
        ones_row = sb("ones_row", [1, P], F32)
        out_bias = sb("out_bias", [P, D], F32)
        u_rows = sb("u_rows", [P, D], F32)
        ident = sb("ident", [P, P], F32)
        bias_cols = sb("bias_cols", [P, 3, KD], F32)
        q_bias = sb("q_bias", [P, KD], F32)
        score_const = sb("score_const", [P, 1], F32)
        score_add = sb("score_add", [P, 1], F32)
        chunk_max = sb("chunk_max", [P, C], F32)
        neg_max = sb("neg_max", [P, 1], F32)
        part_sum = sb("part_sum", [P, E * G], F32)
        den = sb("den", [P, 3], F32)
        stats = sb("stats", [P, 6], F32)
        mean_var = sb("mean_var", [P, 2], F32)
        rs = sb("rs", [P, 4], F32)
        rs_bits = sb("rs_bits", [P, 2], I32)

        ps = [ctx.enter_context(nc.psum_tensor(f"bank{i}", [P, BANK], F32)) for i in range(8)]
        SCORE, PT, O, X, Y, SMALL = 0, 2, 4, 5, 6, 7
        PENALTY_BANKS = (SMALL, Y)
        KEY_BANKS = [PT, PT + 1, O, X]
        M_BANKS = [PT, PT + 1, O, SMALL]

        wq_sb = scores[:, 0:KD * D].rearrange("p (k d) -> p k d", k=KD)
        wk_sb = scores[:, KD * D:2 * KD * D].rearrange("p (k d) -> p k d", k=KD)
        wv_sb = probs[:, 0:KD * D].rearrange("p (k d) -> p k d", k=KD)
        wm_sb = probs[:, KD * D:2 * KD * D].rearrange("p (k d) -> p k d", k=KD)
        spread = pt_hi[:, :, :].rearrange("p a b -> p (a b)").bitcast(F32).rearrange(
            "p (k n) -> p k n", k=KD)
        spread_q = out_bias[:].rearrange("p (k n) -> p k n", k=KD)
        bm_row = pt_lo[0:1, :, :].rearrange("p a b -> p (a b)").bitcast(F32)
        row = v_slots[:, T, :, :].rearrange("p a d -> p (a d)").bitcast(F32)

        def raw(j0, j1):
            return v_slots[:, j0 + 2:j1 + 2, :, :].rearrange("p t a d -> p (t a d)").bitcast(
                F32).rearrange("p (t d) -> p t d", d=D)

        s_wqk = [sem(f"wq_wk_block{k}_loaded") for k in range(KD)]
        s_wvm = sem("wv_wm_loaded")
        s_bias = sem("biases_loaded")
        s_key = [sem(f"key_loaded{g}") for g in range(C)]
        s_val = [sem(f"value_loaded{g}") for g in range(C)]
        s_adj = [sem(f"adj_loaded{i}") for i in range(RING)]
        s_xq = sem("x_query_loaded")
        s_xr = sem("x_res_loaded")
        s_out = sem("out_stored")
        s_ident0 = sem("ident_zeroed")
        s_ident = sem("ident_ready")
        s_fill = sem("spread_filled")
        s_spread = sem("spread_ready")
        s_small_ps = sem("small_vectors_in_psum")
        s_small = sem("small_vectors_ready")
        s_a_ps = sem("a_in_psum")
        s_a_hi = sem("a_hi_ready")
        s_a_lo = sem("a_lo_ready")
        s_key_ps = sem("key_tile_in_psum")
        s_k_hi = sem("k_hi_ready")
        s_k_lo = sem("k_lo_ready")
        s_wmt_ps = sem("wm_transposed_in_psum")
        s_wmt = sem("wm_transposed_ready")
        s_m_ps = sem("m_in_psum")
        s_m_hi = sem("m_hi_ready")
        s_m_lo = sem("m_lo_ready")
        s_ob_ps = sem("out_bias_in_psum")
        s_ob = sem("out_bias_ready")
        s_v_hi = sem("v_hi_ready")
        s_v_lo = sem("v_lo_ready")
        s_xt_ps = sem("x_transposed_in_psum")
        s_xt_hi = sem("xt_hi_ready")
        s_xt_lo = sem("xt_lo_ready")
        s_q_ps = sem("q_in_psum")
        s_q_hi = sem("q_hi_ready")
        s_q_lo = sem("q_lo_ready")
        s_add = sem("score_add_ready")
        s_sc_ps = sem("scores_in_psum")
        s_sc = sem("scores_taken")
        s_abs = sem("abs_ready")
        s_pen = sem("penalty_ready")
        s_masked = sem("scores_masked")
        s_max = sem("max_ready")
        s_exp = sem("exp_ready")
        s_pt = sem("p_transposed")
        s_pt_hi = sem("pt_hi_ready")
        s_pt_lo = sem("pt_lo_ready")
        s_pv = sem("pv_chunk_done")
        s_den = sem("denominator_steps")
        s_row = sem("attention_row_ready")
        s_ot_ps = sem("o_transposed_in_psum")
        s_ot_hi = sem("ot_hi_ready")
        s_ot_lo = sem("ot_lo_ready")
        s_y_ps = sem("projection_in_psum")
        s_ln = [sem(f"layernorm_step{i}") for i in range(LN)]

        def need(eng, s, count):
            if not isinstance(count, int) or count > 0:
                eng.wait_ge(s, count)

        def rows_of(dram, t):
            return dram[bass.ds(t * P, P), :]

        LATE_MASKS = range(2, 5)

        block = ctx.enter_context(nc.Block())

        @block.sync
        def _(sp):
            def load_weights(w, dst, s):
                sp.dma_start(dst, w.rearrange("(k p) d -> p k d", p=P)).then_inc(s, 16)

            def load_block(w, dst, k):
                sp.dma_start(dst[:, k, :], w[k * P:(k + 1) * P, :]).then_inc(s_wqk[k], 16)

            def load_adj(t, c):
                need(sp, s_sc, t * C + c - RING + 1)
                sp.dma_start(adj_in[:, c % RING, :], adj[bass.ds(t * P, P), c * BANK:(c + 1) * BANK]
                             ).then_inc(s_adj[c % RING], 16)

            def load_x_query(t):
                need(sp, s_add, t)
                sp.dma_start(x_query[:], rows_of(x, t)).then_inc(s_xq, 16)

            def load_x_res(t):
                need(sp, s_out, t * 16)
                sp.dma_start(x_res[:], rows_of(x, t)).then_inc(s_xr, 16)

            def store(t):
                sp.wait_ge(s_ln[-1], t + 1)
                sp.dma_start(rows_of(out, t), x_res[:]).then_inc(s_out, 16)

            for k in range(KD):
                load_block(wq, wq_sb, k)
                load_block(wk, wk_sb, k)
            for n, b in enumerate((bq, bk, bv)):
                sp.dma_start(bias_cols[:, n, :], b.rearrange("(k p) -> p k", p=P),
                             allow_slow_non_contiguous=True).then_inc(s_bias, 16)
            sp.dma_start(bm_row, bm.rearrange("(a d) -> a d", a=1)).then_inc(s_bias, 16)
            load_x_query(0)
            for g in range(C):
                sp.dma_start(raw(g * TC, (g + 1) * TC), key[g * BANK:(g + 1) * BANK, :].rearrange(
                    "(t p) d -> p t d", p=P)).then_inc(s_key[g], 16)
                if g < RING:
                    load_adj(0, g)
            load_weights(wv, wv_sb, s_wvm)
            load_weights(wm, wm_sb, s_wvm)
            for g in range(C):
                sp.wait_ge(s_key_ps, (g + 1) * TC)
                sp.dma_start(raw(g * TC, (g + 1) * TC), value[g * BANK:(g + 1) * BANK, :].rearrange(
                    "(t p) d -> p t d", p=P)).then_inc(s_val[g], 16)
                if g + RING < C:
                    load_adj(0, g + RING)
                if g == 2:
                    load_x_query(1)
            load_x_res(0)

            def step(s):
                for c in range(C):
                    load_adj(s, c)
                    if c == RING - 1 and (not isinstance(s, int) or s >= 3):
                        store(s - 3)
                        load_x_res(s - 2)
                if not isinstance(s, int) or s + 1 < T:
                    load_x_query(s + 1)

            for s in range(1, 4):
                step(s)
            with sp.Fori(4, T - 2, 2) as s:
                step(s)
                step(s + 1)
            for s in range(T - 2, T):
                step(s)
            for t in range(T - 3, T):
                store(t)
                if t + 1 < T:
                    load_x_res(t + 1)
            sp.wait_ge(s_out, T * 16)

        @block.gpsimd
        def _(pool):
            pool.memset(ident[:], 0.0).then_inc(s_ident0, 1)
            pool.wait_ge(s_ident0, 1)
            pool.affine_select(out=ident[:], in_=ident[:], compare_op=ALU.not_equal, fill=1.0,
                               base=0, pattern=[[-1, P]], channel_multiplier=1).then_inc(s_ident, 1)
            for j in range(T):
                pool.wait_ge(s_v_hi, j + 1)
                pool.tensor_tensor(v_slots[:, j, 1, :], raw(j, j + 1)[:, 0, :], v_slots[:, j, 0, :],
                                   ALU.subtract).then_inc(s_v_lo, 1)

        @block.tensor
        def _(pe):
            def transpose_blocks(bank, src, s):
                for k in range(KD):
                    last = pe.transpose(ps[bank][:, k * P:(k + 1) * P], src[:, k * P:(k + 1) * P], ident[:])
                last.then_inc(s, 1)

            def products(dst, pairs, first=True, last=True):
                for n, (lh, ll, rh, rl) in enumerate(pairs):
                    pe.matmul(dst, lh, rh, start=first and n == 0, stop=False)
                    pe.matmul(dst, lh, rl, start=False, stop=False)
                    ins = pe.matmul(dst, ll, rh, start=False, stop=last and n == len(pairs) - 1)
                return ins

            def small_vectors():
                pe.wait_ge(s_bias, 64)
                pe.wait_ge(s_spread, 3)
                for dst, lhs, rhs in ((ps[SMALL][:], spread_q, wk_sb), (ps[Y][:], spread, wq_sb),
                                      (ps[O][:, 0:1], spread, bias_cols[:, 0, :])):
                    for k in range(KD):
                        cols = rhs[:, k:k + 1] if dst.shape[-1] == 1 else rhs[:, k, :]
                        ins = pe.matmul(dst, lhs[:, k, :], cols, start=k == 0, stop=k == KD - 1)
                    ins.then_inc(s_small_ps, 1)

            def product_block(bank, left, right, d, k):
                return pe.matmul(ps[bank][:], left[:, k, d * P:(d + 1) * P], right[:, k, :],
                                 start=k == 0, stop=k == KD - 1)

            def product_a():
                for k in range(KD):
                    pe.wait_ge(s_wqk[k], 32)
                    for d in range(KD):
                        ins = product_block(d, wq_sb, wk_sb, d, k)
                        if k == KD - 1:
                            ins.then_inc(s_a_ps, 1)

            def transpose_wm(f):
                for k in range(KD):
                    ins = pe.transpose(ps[M_BANKS[f]][:, k * P:(k + 1) * P],
                                       wm_sb[:, k, f * P:(f + 1) * P], ident[:])
                ins.then_inc(s_wmt_ps, 1)

            def product_m():
                for d in range(KD):
                    if d == KD - 1:
                        pe.wait_ge(s_masked, C)
                    for k in range(KD):
                        if d == 0:
                            pe.wait_ge(s_wmt, k + 1)
                        ins = product_block(M_BANKS[d], wv_sb, wm_sb, d, k)
                    ins.then_inc(s_m_ps, 1)

            def key_tiles(g):
                pe.wait_ge(s_key[g], 16)
                for j in range(g * TC, (g + 1) * TC):
                    need(pe, s_k_lo, j - 3)
                    transpose_blocks(KEY_BANKS[j % 4], raw(j, j + 1)[:, 0, :], s_key_ps)

            def transpose_x(t):
                pe.wait_ge(s_xq, t * 16 + 16)
                transpose_blocks(X, x_query[:], s_xt_ps)

            def query(t):
                pe.wait_ge(s_xt_hi, t + 1)
                pe.wait_ge(s_xt_lo, t + 1)
                for d in range(KD):
                    cut = slice(d * P, (d + 1) * P)
                    ins = products(ps[Y][:, cut], [(a_hi[:, k, cut], a_lo[:, k, cut], xt_hi[:, k, :], xt_lo[:, k, :])
                                                   for k in range(KD)])
                ins.then_inc(s_q_ps, 1)

            def score_chunk(t, c):
                if c == 0:
                    pe.wait_ge(s_q_hi, t * KD + KD)
                    pe.wait_ge(s_q_lo, t * KD + KD)
                need(pe, s_sc, t * C + c - 1)
                cut = slice(c * BANK, (c + 1) * BANK)
                products(ps[SCORE + c % 2][:], [(q_hi[:, k, :], q_lo[:, k, :], k_hi[:, k, cut], k_lo[:, k, cut])
                                                for k in range(KD)]).then_inc(s_sc_ps, 1)

            def pv_chunk(t, c):
                if c == 0:
                    need(pe, s_row, t)
                pe.wait_ge(s_pt_hi, t * C + c + 1)
                pe.wait_ge(s_pt_lo, t * C + c + 1)
                products(ps[O][:], [(pt_hi[:, c % 2, i * P:(i + 1) * P], pt_lo[:, c % 2, i * P:(i + 1) * P],
                                     v_slots[:, c * TC + i, 0, :], v_slots[:, c * TC + i, 1, :])
                                    for i in range(TC)], c == 0, c == C - 1).then_inc(s_pv, 1)

            def transpose_o(t):
                pe.wait_ge(s_row, t + 1)
                transpose_blocks(X, row, s_ot_ps)

            def project(t):
                pe.wait_ge(s_ot_hi, t + 1)
                pe.wait_ge(s_ot_lo, t + 1)
                products(ps[Y][:], [(ot_hi[:, k, :], ot_lo[:, k, :], m_hi[:, k, :], m_lo[:, k, :])
                                    for k in range(KD)]).then_inc(s_y_ps, 1)

            def score_phase(t):
                for c in range(C):
                    score_chunk(t, c)

            def pv_phase(t, next_tile, out_tile):
                for c in range(C):
                    if isinstance(t, int) and t == 0:
                        pe.wait_ge(s_v_hi, (c + 1) * TC)
                        pe.wait_ge(s_v_lo, (c + 1) * TC)
                    pv_chunk(t, c)
                    if out_tile is not None and c == 0:
                        transpose_o(out_tile)
                    if out_tile is not None and c == 2:
                        if not isinstance(t, int) or t + 1 < T:
                            pe.wait_ge(s_masked, t * C + 2 * C)
                        project(out_tile)
                    if next_tile is not None and c == 3:
                        transpose_x(next_tile)
                    if next_tile is not None and c == 5:
                        if out_tile is not None:
                            pe.wait_ge(s_ln[0], out_tile + 1)
                        query(next_tile)

            pe.wait_ge(s_ident, 1)
            product_a()
            transpose_x(0)
            small_vectors()
            pe.wait_ge(s_a_hi, KD)
            pe.wait_ge(s_a_lo, KD)
            pe.wait_ge(s_xt_hi, 1)
            pe.wait_ge(s_xt_lo, 1)
            pe.wait_ge(s_small, 2 + KD)
            key_tiles(0)
            query(0)
            for c in range(C):
                if c + 1 < C:
                    key_tiles(c + 1)
                pe.wait_ge(s_k_hi, (c + 1) * TC)
                pe.wait_ge(s_k_lo, (c + 1) * TC)
                if c == C - 1:
                    transpose_x(1)
                    pe.wait_ge(s_wvm, 32)
                    pe.wait_ge(s_masked, len(LATE_MASKS))
                    for f in range(KD):
                        transpose_wm(f)
                score_chunk(0, c)
            product_m()
            query(1)
            pe.wait_ge(s_spread, 4)
            pe.wait_ge(s_xt_hi, 2)
            pe.wait_ge(s_xt_lo, 2)
            for k in range(KD):
                pe.matmul(ps[X][:], spread[:, k, :], wm_sb[:, k, :], start=k == 0, stop=False)
            pe.matmul(ps[X][:], ones_row[:], bm_row, start=False, stop=True).then_inc(s_ob_ps, 1)
            score_phase(1)
            pe.wait_ge(s_m_hi, KD)
            pe.wait_ge(s_m_lo, KD)
            pe.wait_ge(s_ob, 1)
            pv_phase(0, 2, None)
            with pe.Fori(2, T - 2, 2) as s:
                for i in range(2):
                    score_phase(s + i)
                    pv_phase(s + i - 1, s + i + 1, s + i - 2)
            score_phase(T - 2)
            pv_phase(T - 3, T - 1, T - 4)
            score_phase(T - 1)
            pv_phase(T - 2, None, T - 3)
            pe.wait_ge(s_ln[0], T - 2)
            pv_phase(T - 1, None, T - 2)
            pe.wait_ge(s_ln[0], T - 1)
            transpose_o(T - 1)
            project(T - 1)

        @block.scalar
        def _(act):
            def hi_key(j):
                act.wait_ge(s_key_ps, j + 1)
                act.activation(k_hi[:, :, j * P:(j + 1) * P], ps[KEY_BANKS[j % 4]][:].rearrange("p (k n) -> p k n", k=KD),
                               ACT.Copy).then_inc(s_k_hi, 1)

            def hi_value(j):
                act.wait_ge(s_val[j // TC], 16)
                need(act, s_v_lo, j - 1)
                act.activation(v_slots[:, j, 0, :], raw(j, j + 1)[:, 0, :], ACT.Copy).then_inc(s_v_hi, 1)

            def hi_x(t):
                act.wait_ge(s_xt_ps, t + 1)
                need(act, s_q_ps, t)
                act.activation(xt_hi[:], ps[X][:].rearrange("p (k n) -> p k n", k=KD), ACT.Copy).then_inc(s_xt_hi, 1)

            def hi_query(t):
                act.wait_ge(s_q_ps, t + 1)
                need(act, s_sc_ps, t * C)
                for d in range(KD):
                    act.activation(q_hi[:, d, :], ps[Y][:, d * P:(d + 1) * P], ACT.Identity,
                                   bias=q_bias[:, d:d + 1]).then_inc(s_q_hi, 1)

            def abs_scores(t, c):
                act.wait_ge(s_sc, t * C + c + 1)
                need(act, s_masked, t * C + c - 1)
                act.activation(ps[PENALTY_BANKS[c % 2]][:], scores[:, c * BANK:(c + 1) * BANK], ACT.Abs).then_inc(s_abs, 1)

            def exps(t, n0, n1):
                for n in range(n0, n1):
                    e, b, g = n // (G * G), n // G % G, n % G
                    if n == 0:
                        act.wait_ge(s_max, t + 1)
                        need(act, s_den, t * 3 - 2)
                    if n % (G * G) == 0:
                        need(act, s_pt, (t - 1) * C + EDGES[e + 1])
                    cut = slice(EDGES[e] * BANK, EDGES[e + 1] * BANK)
                    src = scores[b * Q:(b + 1) * Q, cut].rearrange("p (i g k) -> p i g k", g=G, k=Q)
                    dst = probs[g * Q:(g + 1) * Q, cut].rearrange("p (i b k) -> p i b k", b=G, k=Q)
                    ins = act.activation(dst[:, :, b, :], src[:, :, g, :], ACT.Exp,
                                         bias=neg_max[b * Q:(b + 1) * Q, 0:1],
                                         accum_out=part_sum[b * Q:(b + 1) * Q, e * G + g:e * G + g + 1])
                    if n % (G * G) == G * G - 1:
                        ins.then_inc(s_exp, 1)

            def hi_p(t, c):
                act.wait_ge(s_pt, t * C + c + 1)
                need(act, s_pv, t * C + c - 1)
                act.activation(pt_hi[:, c % 2, :], ps[PT + c % 2][:], ACT.Copy, scale=PS).then_inc(s_pt_hi, 1)

            def attention_row(t):
                act.wait_ge(s_pv, t * C + C)
                act.wait_ge(s_den, t * 3 + 3)
                need(act, s_ot_ps, t)
                act.activation(row, ps[O][:], ACT.Copy, scale=den[:, 2:3]).then_inc(s_row, 1)

            def hi_o(t):
                act.wait_ge(s_ot_ps, t + 1)
                act.activation(ot_hi[:], ps[X][:].rearrange("p (k n) -> p k n", k=KD), ACT.Copy).then_inc(s_ot_hi, 1)

            IN_PV = (0, 0, 2, 5, 10, 12, 15, 18, 22)
            IN_SCORES = (25, 28, 30, PARTS)

            def score_phase(t, exp_tile):
                for c in range(C):
                    if exp_tile is not None and c < len(IN_SCORES):
                        exps(exp_tile, (IN_PV[-1:] + IN_SCORES)[c], IN_SCORES[c])
                    abs_scores(t, c)
                    if c == C - 4:
                        hi_p(t - 1, 0)
                    if c == C - 3:
                        hi_p(t - 1, 1)

            def pv_phase(t, next_tile, query_tile, out_tile, marks=IN_PV, ahead=None):
                for c in range(1, C):
                    if c > 1:
                        hi_p(t, c)
                    if query_tile is not None and c == 5:
                        hi_x(query_tile)
                    if next_tile is not None:
                        exps(next_tile, marks[c - 1], marks[c])
                    if out_tile is not None and c == 1:
                        hi_o(out_tile)
                    if query_tile is not None and c == C - 1:
                        hi_query(query_tile)
                if next_tile is not None:
                    exps(next_tile, marks[C - 1], marks[C])
                if ahead is not None:
                    hi_p(ahead, 0)
                attention_row(t)
                if ahead is not None:
                    hi_p(ahead, 1)

            for d in range(KD):
                act.wait_ge(s_a_ps, d + 1)
                act.activation(a_hi[:, d, :], ps[d][:], ACT.Copy, scale=WS).then_inc(s_a_hi, 1)
            hi_x(0)
            values = iter(range(T))

            def hi_values(n):
                for _, j in zip(range(n), values):
                    hi_value(j)

            for g in range(C):
                for j in range(g * TC, (g + 1) * TC):
                    hi_key(j)
                if g == 0:
                    act.wait_ge(s_small, 2 + KD)
                    hi_query(0)
                if g >= 2:
                    hi_values(1 if g == C - 2 else 3)
                if g in LATE_MASKS:
                    abs_scores(0, g - LATE_MASKS[0])
            hi_x(1)
            act.wait_ge(s_wmt, KD)
            for c in range(len(LATE_MASKS), C):
                abs_scores(0, c)
                hi_values(1)
            hi_values(6)
            act.wait_ge(s_m_ps, KD)
            exps(0, 0, 4)
            hi_query(1)
            exps(0, 4, G * G)
            act.wait_ge(s_ob_ps, 1)
            act.wait_ge(s_m_lo, KD)
            for c in range(C):
                if c < 4:
                    exps(0, G * G + c * G, G * G + (c + 1) * G)
                abs_scores(1, c)
                if c == C - 4:
                    hi_p(0, 0)
                if c == C - 3:
                    hi_p(0, 1)
                if c >= 4:
                    hi_values(2)
            pv_phase(0, 1, 2, None)
            with act.Fori(2, T - 2, 2) as s:
                for i in range(2):
                    score_phase(s + i, s + i - 1)
                    pv_phase(s + i - 1, s + i, s + i + 1, s + i - 2)
            score_phase(T - 2, T - 3)
            pv_phase(T - 3, T - 2, T - 1, T - 4)
            score_phase(T - 1, T - 2)
            pv_phase(T - 2, T - 1, None, T - 3, marks=IN_PV[:-1] + IN_PV[-2:-1], ahead=T - 1)
            pv_phase(T - 1, T - 1, None, T - 2, marks=IN_PV[-2:-1] + (22, 27) + (PARTS,) * (C - 2))
            hi_o(T - 1)

        @block.vector
        def _(dve):
            def lo_key(j):
                dve.wait_ge(s_k_hi, j + 1)
                cut = slice(j * P, (j + 1) * P)
                dve.tensor_tensor(k_lo[:, :, cut], ps[KEY_BANKS[j % 4]][:].rearrange("p (k n) -> p k n", k=KD),
                                  k_hi[:, :, cut], ALU.subtract).then_inc(s_k_lo, 1)

            def lo_weights(hi, lo, d, bank, s_hi, s_lo):
                dve.wait_ge(s_hi, d + 1)
                dve.scalar_tensor_tensor(lo[:, d, :], ps[bank][:], WS, hi[:, d, :], ALU.mult,
                                         ALU.subtract).then_inc(s_lo, 1)

            def lo_x(t):
                dve.wait_ge(s_xt_hi, t + 1)
                dve.tensor_tensor(xt_lo[:], ps[X][:].rearrange("p (k n) -> p k n", k=KD), xt_hi[:],
                                  ALU.subtract).then_inc(s_xt_lo, 1)

            def row_constant(t):
                dve.tensor_tensor_reduce(out=x_query[:], in0=x_query[:], in1=u_rows[:], scale=1.0,
                                         scalar=score_const[:, 0:1], op0=ALU.mult, op1=ALU.add,
                                         accum_out=score_add[:, 0:1]).then_inc(s_add, 1)

            def lo_query(t):
                dve.wait_ge(s_q_hi, t * KD + KD)
                for d in range(KD):
                    dve.scalar_tensor_tensor(q_lo[:, d, :], ps[Y][:, d * P:(d + 1) * P], q_bias[:, d:d + 1],
                                             q_hi[:, d, :], ALU.add, ALU.subtract).then_inc(s_q_lo, 1)

            def take_scores(t, c):
                if c == 0:
                    dve.wait_ge(s_add, t + 1)
                if c in EDGES:
                    need(dve, s_exp, (t - 1) * E + EDGES.index(c) + 1)
                dve.wait_ge(s_sc_ps, t * C + c + 1)
                dve.wait_ge(s_adj[c % RING], t * (C // RING * 16) + (c // RING + 1) * 16)
                dve.scalar_tensor_tensor(scores[:, c * BANK:(c + 1) * BANK], ps[SCORE + c % 2][:],
                                         score_add[:, 0:1], adj_in[:, c % RING, :],
                                         ALU.add, ALU.mult).then_inc(s_sc, 1)

            def penalties(t, c):
                dve.wait_ge(s_abs, t * C + c + 1)
                bank = ps[PENALTY_BANKS[c % 2]]
                dve.tensor_scalar(bank[:], bank[:], NEAR_ZERO, PENALTY, ALU.is_lt, ALU.mult).then_inc(s_pen, 1)

            def mask_chunk(t, c):
                cut = scores[:, c * BANK:(c + 1) * BANK]
                dve.wait_ge(s_add, 1)
                if c == 0:
                    need(dve, s_max, t)
                dve.wait_ge(s_pen, t * C + c + 1)
                dve.wait_ge(s_sc, t * C + c + 1)
                dve.tensor_tensor_reduce(out=cut, in0=cut, in1=ps[PENALTY_BANKS[c % 2]][:], scale=TO_SCORE, scalar=-3e38,
                                         op0=ALU.add, op1=ALU.max, accum_out=chunk_max[:, c:c + 1]
                                         ).then_inc(s_masked, 1)

            def row_max(t):
                dve.wait_ge(s_masked, t * C + C)
                need(dve, s_exp, t * E)
                dve.tensor_reduce(neg_max[:], chunk_max[:], AX_X, ALU.max, negate=True).then_inc(s_max, 1)

            def denominator(t):
                dve.wait_ge(s_exp, t * E + E)
                need(dve, s_row, t)
                dve.tensor_reduce(den[:, 0:1], part_sum[:], AX_X, ALU.add).then_inc(s_den, 1)
                dve.wait_ge(s_den, t * 3 + 1)
                dve.tensor_scalar(den[:, 1:2], den[:, 0:1], PS, None, ALU.mult).then_inc(s_den, 1)
                dve.wait_ge(s_den, t * 3 + 2)
                dve.reciprocal(den[:, 2:3], den[:, 1:2]).then_inc(s_den, 1)

            def transpose_p(t, c):
                if c in EDGES:
                    dve.wait_ge(s_exp, t * E + EDGES.index(c) + 1)
                need(dve, s_pt_lo, t * C + c - 1)
                dve.transpose(ps[PT + c % 2][:], probs[:, c * BANK:(c + 1) * BANK]).then_inc(s_pt, 1)

            def lo_p(t, c):
                dve.wait_ge(s_pt_hi, t * C + c + 1)
                dve.scalar_tensor_tensor(pt_lo[:, c % 2, :], ps[PT + c % 2][:], PS, pt_hi[:, c % 2, :],
                                         ALU.mult, ALU.subtract).then_inc(s_pt_lo, 1)

            def lo_o(t):
                dve.wait_ge(s_ot_hi, t + 1)
                dve.tensor_tensor(ot_lo[:], ps[X][:].rearrange("p (k n) -> p k n", k=KD), ot_hi[:],
                                  ALU.subtract).then_inc(s_ot_lo, 1)

            def after(n, t):
                dve.wait_ge(s_add, 1)
                dve.wait_ge(s_ln[n], t + 1)

            var = mean_var[:, 1:2]
            shifted, seed = rs_bits[:, 0:1], rs_bits[:, 1:2]
            veps, half, guess, work = (rs[:, i:i + 1] for i in range(4))

            def add_residual(t):
                dve.wait_ge(s_y_ps, t + 1)
                dve.wait_ge(s_xr, t * 16 + 16)
                dve.scalar_tensor_tensor(x_res[:], ps[Y][:], 1.0 / WS, x_res[:], ALU.mult,
                                         ALU.add).then_inc(s_ln[0], 1)

            def row_statistics(t):
                after(0, t)
                dve.tensor_tensor(x_res[:], x_res[:], out_bias[:], ALU.add).then_inc(s_ln[1], 1)
                after(1, t)
                dve.bn_stats(stats[:], x_res[:]).then_inc(s_ln[2], 1)

            def rsqrt_guess(t):
                after(2, t)
                dve.bn_aggr(mean_var[:], stats[:]).then_inc(s_ln[3], 1)
                after(3, t)
                dve.tensor_scalar(veps, var, EPS, None, ALU.add).then_inc(s_ln[4], 1)
                after(4, t)
                dve.tensor_scalar(half, veps, -0.5, None, ALU.mult).then_inc(s_ln[5], 1)
                dve.tensor_scalar(shifted, veps.bitcast(I32), 1, None,
                                  ALU.logical_shift_right).then_inc(s_ln[6], 1)
                after(6, t)
                dve.tensor_scalar(seed, shifted, -1.0, RSQRT_SEED, ALU.mult, ALU.add).then_inc(s_ln[7], 1)

            def newton(t, n):
                cur = guess if n else seed.bitcast(F32)
                after(7 + 2 * n, t)
                if n == 0:
                    after(5, t)
                dve.scalar_tensor_tensor(work, cur, half, cur, ALU.mult, ALU.mult).then_inc(s_ln[8 + 2 * n], 1)
                after(8 + 2 * n, t)
                dve.scalar_tensor_tensor(guess, work, 1.5, cur, ALU.add, ALU.mult).then_inc(s_ln[9 + 2 * n], 1)

            def normalize(t):
                after(LN - 2, t)
                dve.tensor_scalar(x_res[:], x_res[:], mean_var[:, 0:1], guess, ALU.subtract,
                                  ALU.mult).then_inc(s_ln[LN - 1], 1)

            def score_phase(t):
                for c in range(C):
                    if c > 0:
                        penalties(t, c - 1)
                    take_scores(t, c)
                    if c > 0:
                        mask_chunk(t, c - 1)
                    if C - 5 <= c < C - 3:
                        transpose_p(t - 1, c - C + 5)
                    if C - 3 <= c < C - 1:
                        lo_p(t - 1, c - C + 3)
                transpose_p(t - 1, 2)
                penalties(t, C - 1)
                mask_chunk(t, C - 1)
                row_max(t)
                denominator(t - 1)
                transpose_p(t - 1, 3)

            def pv_phase(t, next_tile, out_tile, ahead=None):
                last = isinstance(t, int) and t == T - 1
                lead = 1 if last else 2
                for c in range(2, C):
                    lo_p(t, c)
                    if ahead is not None and c >= C - 2:
                        transpose_p(ahead, c - C + 2)
                    if last and c == 4:
                        denominator(t)
                    if EDGES[1] <= c + lead < C:
                        transpose_p(t, c + lead)
                    if next_tile is not None and c == 5:
                        lo_x(next_tile)
                    if out_tile is not None:
                        if c == 2:
                            lo_o(out_tile)
                        if c == 4:
                            add_residual(out_tile)
                        if c == 5:
                            row_statistics(out_tile)
                        if c == 6:
                            rsqrt_guess(out_tile)
                        if c == 7:
                            newton(out_tile, 0)
                if next_tile is not None:
                    lo_query(next_tile)
                if ahead is not None:
                    for c in range(2):
                        lo_p(ahead, c)
                        transpose_p(ahead, c + 2)
                if out_tile is not None:
                    newton(out_tile, 1)
                    newton(out_tile, 2)
                if next_tile is not None:
                    row_constant(next_tile)
                if out_tile is not None:
                    normalize(out_tile)

            def spread_bias(n, dst, filled):
                dve.memset(dst, 1.0).then_inc(s_fill, 1)
                dve.wait_ge(s_fill, filled)
                for k in range(KD):
                    ins = dve.tensor_scalar(dst[:, k, :], dst[:, k, :], bias_cols[:, n, k:k + 1], None, ALU.mult)
                ins.then_inc(s_spread, 1)

            def copy_wm(f):
                dve.wait_ge(s_wmt_ps, KD)
                dve.tensor_copy(wm_sb[:, f, :], ps[M_BANKS[f]][:]).then_inc(s_wmt, 1)

            dve.memset(ones_row[:], 1.0).then_inc(s_spread, 1)
            dve.wait_ge(s_bias, 64)
            spread_bias(1, spread, 1)
            spread_bias(0, spread_q, 2)
            for d in range(KD):
                lo_weights(a_hi, a_lo, d, d, s_a_hi, s_a_lo)
            lo_x(0)
            dve.wait_ge(s_ident, 1)
            dve.wait_ge(s_small_ps, 1)
            for d in range(KD):
                cut = slice(d * P, (d + 1) * P)
                dve.tensor_tensor_reduce(out=x_res[:, cut], in0=ps[SMALL][:, cut], in1=ident[:], scale=WS,
                                         scalar=0.0, op0=ALU.mult, op1=ALU.add,
                                         accum_out=q_bias[:, d:d + 1]).then_inc(s_small, 1)
            dve.wait_ge(s_small_ps, 2)
            dve.tensor_scalar(u_rows[:], ps[Y][:], WS, None, ALU.mult).then_inc(s_small, 1)
            dve.wait_ge(s_small_ps, 3)
            dve.tensor_scalar(score_const[:], ps[O][:, 0:1], WS, None, ALU.mult).then_inc(s_small, 1)
            for j in range(TC):
                lo_key(j)
            lo_query(0)
            dve.wait_ge(s_small, 2 + KD)
            row_constant(0)
            spread_bias(2, spread, 3)
            for c in range(C):
                if c + 1 < C:
                    for j in range((c + 1) * TC, (c + 2) * TC):
                        lo_key(j)
                if c == C - 1:
                    lo_x(1)
                    for f in range(KD):
                        copy_wm(f)
                take_scores(0, c)
                if c in LATE_MASKS:
                    penalties(0, c - LATE_MASKS[0])
                    mask_chunk(0, c - LATE_MASKS[0])
            for c in range(len(LATE_MASKS), C):
                penalties(0, c)
                mask_chunk(0, c)
            row_max(0)
            row_constant(1)
            for d in range(KD):
                dve.wait_ge(s_m_ps, d + 1)
                dve.tensor_scalar(m_hi[:, d, :], ps[M_BANKS[d]][:], WS, None, ALU.mult).then_inc(s_m_hi, 1)
                lo_weights(m_hi, m_lo, d, M_BANKS[d], s_m_hi, s_m_lo)
            lo_query(1)
            dve.wait_ge(s_ob_ps, 1)
            dve.tensor_copy(out_bias[:], ps[X][:]).then_inc(s_ob, 1)
            score_phase(1)
            pv_phase(0, 2, None)
            with dve.Fori(2, T - 2, 2) as s:
                for i in range(2):
                    score_phase(s + i)
                    pv_phase(s + i - 1, s + i + 1, s + i - 2)
            score_phase(T - 2)
            pv_phase(T - 3, T - 1, T - 4)
            score_phase(T - 1)
            pv_phase(T - 2, None, T - 3, ahead=T - 1)
            pv_phase(T - 1, None, T - 2)
            lo_o(T - 1)
            add_residual(T - 1)
            row_statistics(T - 1)
            rsqrt_guess(T - 1)
            for n in range(3):
                newton(T - 1, n)
            normalize(T - 1)


_INS = ["x", "adj", "L0_gnn_key", "L0_gnn_value", "L0_gnn_Wq", "L0_gnn_bq", "L0_gnn_Wk", "L0_gnn_bk",
        "L0_gnn_Wv", "L0_gnn_bv", "L0_gnn_Wm", "L0_gnn_bm"]


def kernel(**inputs):
    import concourse.bacc as bacc
    from concourse.bass_utils import run_bass_kernel_spmd

    nc = bacc.Bacc("TRN2", target_bir_lowering=False, num_devices=1)
    arrays, args = {}, []
    for name in _INS:
        a = np.ascontiguousarray(inputs[name])
        arrays[f"in_{name}_dram"] = a
        args.append(nc.dram_tensor(f"in_{name}_dram", a.shape, mybir.dt.from_np(a.dtype), kind="ExternalInput").ap())
    out = nc.dram_tensor("out_dram", inputs["x"].shape, F32, kind="ExternalOutput").ap()
    attention_resnorm(nc, *args, out)
    r = run_bass_kernel_spmd(nc, [arrays], core_ids=[0])
    return r.results[0]["out_dram"]
```
